# Optimizing a Trainium2 kernel written in Bass

```python
import numpy as np
import jax
import jax.numpy as jnp

def _softmax(x, axis=-1):
    return jax.nn.softmax(x, axis=axis)

def _gelu(x):
    return jax.nn.gelu(x, approximate=True)

def _silu(x):
    return jax.nn.silu(x)

def _sigmoid(x):
    return jax.nn.sigmoid(x)

def _layernorm(x, axis=-1, eps=1e-05):
    m = jnp.mean(x, axis=axis, keepdims=True)
    v = jnp.var(x, axis=axis, keepdims=True)
    return (x - m) / jnp.sqrt(v + eps)

def _scatter_add(tgt, idx, src, axis=0):
    return tgt.at[idx].add(src)

def _segment_sum(src, seg, n):
    return jax.ops.segment_sum(src, seg, n)
kernel_name = 'mk_prb_d1_jaxref_r4_ad87c6'

def setup_inputs(seed: int=0):
    np.random.seed(seed)
    _w = jnp.asarray

    def _L0_attn_setup():
        import jax, jax.numpy as jnp
        import numpy as np
        N_EMBD = 256
        N_HEAD = 8
        HEAD_DIM = N_EMBD // N_HEAD
        EPS = 1e-06

        def _lrpe(xh, theta, n):
            idx = jnp.arange(n, dtype=xh.dtype).reshape(1, n, 1)
            th = theta * idx
            th = th[None]
            return jnp.concatenate([xh * jnp.cos(th), xh * jnp.sin(th)], axis=-1)

        def _srmsnorm(y):
            ms = jnp.mean(jnp.square(y), axis=-1, keepdims=True)
            return y * jax.lax.rsqrt(ms + EPS)
        key = jax.random.key(seed)
        ks = jax.random.split(key, 8)
        b, n = (2, 512)
        x = jax.random.normal(ks[0], (b, n, N_EMBD), dtype=jnp.float32)
        slope_rate = -jax.random.uniform(ks[1], (N_HEAD, 1, 1), dtype=jnp.float32)
        s = 0.02
        qkvu_w = jax.random.normal(ks[2], (4 * N_EMBD, N_EMBD), dtype=jnp.float32) * s
        qkvu_b = jnp.zeros((4 * N_EMBD,), dtype=jnp.float32)
        out_w = jax.random.normal(ks[3], (N_EMBD, N_EMBD), dtype=jnp.float32) * s
        out_b = jnp.zeros((N_EMBD,), dtype=jnp.float32)
        d = N_EMBD
        theta = (10000.0 ** (-2.0 / d * jnp.arange(d, dtype=jnp.float32))).reshape(N_HEAD, 1, HEAD_DIM)
        return {'x': x, 'slope_rate': slope_rate, 'qkvu_w': qkvu_w, 'qkvu_b': qkvu_b, 'out_w': out_w, 'out_b': out_b, 'theta': theta}
    _L0_attn_in = _L0_attn_setup()

    def _L0_ffn_setup():
        import jax, jax.numpy as jnp
        import numpy as np
        B, S, H, F, E = (2, 512, 256, 1024, 8)
        key = jax.random.key(seed)
        ks = jax.random.split(key, 4)
        x = jax.random.normal(ks[0], (B, S, H), dtype=jnp.float32)
        w_router = jax.random.normal(ks[1], (H, E), dtype=jnp.float32) * 0.02
        w1 = jax.random.normal(ks[2], (E, H, F), dtype=jnp.float32) * 0.02
        b1 = jnp.zeros((E, F), dtype=jnp.float32)
        w2 = jax.random.normal(ks[3], (E, F, H), dtype=jnp.float32) * 0.02
        b2 = jnp.zeros((E, H), dtype=jnp.float32)
        return {'x': x, 'w_router': w_router, 'w1': w1, 'b1': b1, 'w2': w2, 'b2': b2}
    _L0_ffn_in = _L0_ffn_setup()
    _d = {'L0_attn_x': _L0_attn_in['x'], 'L0_attn_slope_rate': _L0_attn_in['slope_rate'], 'L0_attn_qkvu_w': _L0_attn_in['qkvu_w'], 'L0_attn_qkvu_b': _L0_attn_in['qkvu_b'], 'L0_attn_out_w': _L0_attn_in['out_w'], 'L0_attn_out_b': _L0_attn_in['out_b'], 'L0_attn_theta': _L0_attn_in['theta'], 'L0_ffn_w_router': _L0_ffn_in['w_router'], 'L0_ffn_w1': _L0_ffn_in['w1'], 'L0_ffn_b1': _L0_ffn_in['b1'], 'L0_ffn_w2': _L0_ffn_in['w2'], 'L0_ffn_b2': _L0_ffn_in['b2']}
    _x0 = _d['L0_attn_x']
    _d['L0_attn_x'] = jax.random.normal(jax.random.fold_in(jax.random.key(seed), 1), (2, 2048, 256), dtype=_x0.dtype)
    del _x0
    return _d

def reference(L0_attn_x, L0_attn_slope_rate, L0_attn_qkvu_w, L0_attn_qkvu_b, L0_attn_out_w, L0_attn_out_b, L0_attn_theta, L0_ffn_w_router, L0_ffn_w1, L0_ffn_b1, L0_ffn_w2, L0_ffn_b2):

    def _L0_attn_ref(x, slope_rate, qkvu_w, qkvu_b, out_w, out_b, theta):
        import jax, jax.numpy as jnp
        import numpy as np
        N_EMBD = 256
        N_HEAD = 8
        HEAD_DIM = N_EMBD // N_HEAD
        EPS = 1e-06

        def _lrpe(xh, theta, n):
            idx = jnp.arange(n, dtype=xh.dtype).reshape(1, n, 1)
            th = theta * idx
            th = th[None]
            return jnp.concatenate([xh * jnp.cos(th), xh * jnp.sin(th)], axis=-1)

        def _srmsnorm(y):
            ms = jnp.mean(jnp.square(y), axis=-1, keepdims=True)
            return y * jax.lax.rsqrt(ms + EPS)
        b, n, hd = x.shape
        h = N_HEAD
        qkvu = x @ qkvu_w.T + qkvu_b
        q, k, v, u = jnp.split(qkvu, 4, axis=-1)

        def to_heads(t):
            return t.reshape(b, n, h, hd // h).transpose(0, 2, 1, 3)
        q, k, v = (to_heads(q), to_heads(k), to_heads(v))
        q = jax.nn.silu(q)
        k = jax.nn.silu(k)
        q = _lrpe(q, theta, n)
        k = _lrpe(k, theta, n)
        tril = jnp.tril(jnp.ones((n, n), dtype=x.dtype))
        mask = jnp.exp(slope_rate * tril)
        energy = jnp.einsum('bhne,bhme->bhnm', q, k) * mask[None]
        out = jnp.einsum('bhnm,bhmd->bhnd', energy, v)
        out = out.transpose(0, 2, 1, 3).reshape(b, n, hd)
        out = _srmsnorm(out)
        out = u * out
        out = out @ out_w.T + out_b
        return out

    def _L0_ffn_ref(x, w_router, w1, b1, w2, b2):
        import jax, jax.numpy as jnp
        import numpy as np
        B, S, H, F, E = (2, 512, 256, 1024, 8)
        'Top-1 MoE layer: route -> per-expert FFN -> weighted combine.\n\n            Faithful to ExpertParallelWrapper._process_moe_layer on a single group:\n            router picks one expert per token with a routing weight; tokens are\n            dispatched to experts (here expressed as a static mask over the fixed\n            expert set), processed by the expert FFN, and scatter-combined back\n            weighted by the routing probability.\n            '
        Bs, Ss, Hs = x.shape
        n_experts = w1.shape[0]
        logits = jnp.einsum('bsh,he->bse', x, w_router)
        probs = jax.nn.softmax(logits, axis=-1)
        sel = jnp.argmax(probs, axis=-1)
        wgt = jnp.take_along_axis(probs, sel[..., None], axis=-1)[..., 0]
        xt = x.reshape(-1, Hs)
        sel_t = sel.reshape(-1)
        wgt_t = wgt.reshape(-1)
        out = jnp.zeros_like(xt)
        for e in range(n_experts):
            h = jax.nn.relu(xt @ w1[e] + b1[e])
            y = h @ w2[e] + b2[e]
            m = (sel_t == e).astype(xt.dtype) * wgt_t
            out = out + m[:, None] * y
        return out.reshape(Bs, Ss, Hs)
    x = L0_attn_x
    xn = _layernorm(x, axis=-1)
    x = x + _L0_attn_ref(xn, L0_attn_slope_rate, L0_attn_qkvu_w, L0_attn_qkvu_b, L0_attn_out_w, L0_attn_out_b, L0_attn_theta) + _L0_ffn_ref(xn, L0_ffn_w_router, L0_ffn_w1, L0_ffn_b1, L0_ffn_w2, L0_ffn_b2)
    return x

_drawn_inputs = setup_inputs


def setup_inputs(seed=0):
    import zlib

    import numpy as np

    out = dict(_drawn_inputs(seed))
    spreads = {'L0_attn_qkvu_b': (0.0, 0.1),
     'L0_attn_out_b': (0.0, 0.1),
     'L0_ffn_b1': (0.0, 0.8),
     'L0_ffn_b2': (0.0, 0.41)}
    factors = {'L0_attn_slope_rate': 4.681}
    for name, (base, spread) in spreads.items():
        noise = np.random.default_rng([zlib.crc32(name.encode()), seed]).standard_normal(out[name].shape)
        drawn = base * np.exp(spread * noise) if base else spread * noise
        out[name] = jnp.asarray(drawn.astype(out[name].dtype))
    for name, factor in factors.items():
        out[name] = (out[name] * factor).astype(out[name].dtype)
    return out
```

```python
from contextlib import ExitStack

import numpy as np
import concourse.bass as bass
from concourse import mybir

F32 = mybir.dt.float32
BF16 = mybir.dt.bfloat16
I32 = mybir.dt.int32
U32 = mybir.dt.uint32
ALU = mybir.AluOpType
ACT = mybir.ActivationFunctionType
AX = mybir.AxisListType

P = 128
BATCH, SEQ, D = 2, 2048, 256
HEADS, HD = 8, 32
EXPERTS, FF = 8, 1024
KC = D // P
CHUNKS = SEQ // P
TILES = BATCH * CHUNKS
FC = FF // P
SORTED = TILES + EXPERTS - 1
ROW = D + 2
NOBODY = 1 << 20
LN_EPS = 1e-5
RMS_EPS = 1e-6
TWO_PI_A = 6.28125
TWO_PI_B = float(np.float32(0.0019350051879882812))
TWO_PI_C = float(2 * np.pi - TWO_PI_A - TWO_PI_B)
ROUND = 1.5 * 2.0 ** 23
PI_IN = 3.1415925
WSIZE = KC * FF + FC * D


def need(engine, sem, count):
    if not isinstance(count, int) or count > 0:
        engine.wait_ge(sem, count)


def build(nc, x, slope, wqkvu, bqkvu, wout, bout, theta, bu_cols, w1, b1, w2, b2, out, xn_d, sorted_d):
    ctx = ExitStack()
    with ctx:
        def sb(name, cols, dt=F32):
            return ctx.enter_context(nc.sbuf_tensor(name, [P, cols], dt))

        def sem(name):
            return ctx.enter_context(nc.semaphore(name))

        region = sb("region", EXPERTS * WSIZE)
        at = [0]

        def part(cols):
            at[0] += cols
            return region[:, at[0] - cols:at[0]]

        kT_all = part(CHUNKS * 512)
        v_all = part(CHUNKS * D)
        xT_all = part(CHUNKS * D)
        cos_all = part(CHUNKS * D)
        sin_all = part(CHUNKS * D)
        states = part((CHUNKS + 1) * D)
        trig = part(3 * 1024)
        kT_now = part(512)
        v_now = part(D)
        assert at[0] <= EXPERTS * WSIZE
        xT_now = sb("xT_now", 2 * D)

        masked = trig[:, 0:2 * HEADS * P]
        qT = trig[:, 2 * HEADS * P:2 * HEADS * P + 2 * 512]

        xy = sb("xy", TILES * D)
        work = sb("work", 5648)
        wproj, wo_sb, mask, wstate, wterm, rot = (work[:, a:b] for a, b in (
            (0, 2064), (2064, 2576), (2576, 3600), (3600, 4112), (4112, 4624), (4624, 5648)))
        b1_p = work[:, 0:4096].bitcast(BF16)
        b2_p = work[:, 4096:5120].bitcast(BF16)
        small = sb("small", 1792)
        xn, act_k, oT, osq, zT = (small[:, a:b] for a, b in (
            (0, 512), (512, 1024), (1024, 1280), (1280, 1536), (1536, 1792)))
        qbd = sb("qbd", 4 * ROW)
        es_row = sb("es_row", D)
        bout_row = sb("bout_row", D)
        theta_row = rot[:, 0:D]
        ident = sb("ident", P)
        ones = sb("ones", P)
        upper = sb("upper", P)
        ones_b = sb("ones_b", P, BF16)
        bqkv_p = sb("bqkv_p", 776, BF16)
        bu_col = sb("bu_col", KC)
        stats = sb("stats", 6 * TILES)
        mv = sb("mv", 2 * TILES)
        rstd = sb("rstd", TILES)
        slope_bc = sb("slope_bc", HEADS)
        es = sb("es", HEADS)
        pos0 = sb("pos0", CHUNKS)
        ms = sb("ms", TILES)
        logits = sb("logits", TILES * EXPERTS)
        posi = sb("posi", TILES, U32)
        experts_i = sb("experts_i", SORTED, I32)
        tag = sb("tag", 2 * TILES)
        ini = sb("ini", CHUNKS, I32)
        pad_row = wterm[:, 0:ROW]
        ids = sb("ids", 4, U32)
        halfpi = sb("halfpi", 1)

        ps = [ctx.enter_context(nc.psum_tensor(f"bank{i}", [P, 512], F32)) for i in range(8)]

        names = """const_in xn_ready xT_psum xT_ready kv_psum k_act kv_free v_ready rope_k kT_psum kT_ready k_now v_now xT_kept
            state_psum state_ready lg_ready pad_set pad_out q_psum q_act rope_q qT_psum q_moved s_psum s_masked
            w_part w_ready u_psum o_psum o_moved z_ready y_psum y_moved gp_const stat_a stat_b stat_c tab mask_part rows
            bias_t attn_out attn_row route_a route_act route_pe route_b disp_tag disp_out
            wt_in xt_psum xt_ready h_psum h_ready hT_psum hT_ready ye_psum ye_ready ids_ready ln_part""".split()
        S = {n: sem(n) for n in names}
        for n in ("xr_in", "xs_in", "disp_in", "disp_out", "x_in", "b_in", "x_now", "xn_out", "ye_out"):
            S[n] = [sem(f"{n}{k}") for k in range(8 if n == "x_in" else 4)]
        xs_buf = [xy[:, k * ROW:(k + 1) * ROW] for k in range(4)]
        moe_xT = [xy[:, 2048 + k * D:2048 + (k + 1) * D] for k in range(2)]
        moe_h = xy[:, 3072:4096]
        moe_hT = xy[:, 4096:5120]
        moe_y = [xy[:, 5120 + k * D:5120 + (k + 1) * D] for k in range(4)]
        disp = [qbd[:, k * ROW:(k + 1) * ROW] for k in range(4)]

        block = ctx.enter_context(nc.Block())

        def view(t, off, cols):
            return t[:, bass.ds(off, cols)]

        def steps(eng, n, lead, lag, step):
            first = lag + (lag & 1)
            last = n - lead - ((n - lead - first) & 1)
            for t in range(-lead, first):
                step(t, t & 1)
            with eng.Fori(0, (last - first) // 2) as k:
                i = k * 2 + first
                step(i, 0)
                step(i + 1, 1)
            for t in range(last, n + lag):
                step(t, t & 1)

        def live(t, n):
            return not isinstance(t, int) or 0 <= t < n

        @block.sync
        def _(sp):
            for t in range(0, TILES, 4):
                sp.dma_start(xy[:, t * D:(t + 4) * D].rearrange("p (t d) -> p t d", d=D),
                             x[t * P:(t + 4) * P, :].rearrange("(t p) d -> p t d", p=P)).then_inc(S["x_in"][t // 4], 16)
            sp.wait_ge(S["pad_set"], 2)
            with sp.Fori(0, SORTED) as j:
                sp.dma_start(sorted_d[bass.ds(j * P, P), :], pad_row[:, :]).then_inc(S["pad_out"], 16)
            for b in range(BATCH):
                with sp.Fori(0, CHUNKS // 2) as k:
                    for par in range(2):
                        g = b * CHUNKS + k * 2 + par
                        sp.wait_ge(S["xn_ready"], g + 1)
                        sp.dma_start(xn_d[bass.ds(g * P, P), :], xn[:, par * D:(par + 1) * D]).then_inc(S["xn_out"][par], 16)

                def stage(t, par, b=b):
                    i = t + 1
                    if live(i, CHUNKS):
                        g = b * CHUNKS + i
                        need(sp, S["q_psum"], g - 1)
                        sp.dma_start(xT_now[:, (1 - par) * D:(2 - par) * D], view(xT_all, i * D, D)).then_inc(S["x_now"][1 - par], 16)
                    if live(t, CHUNKS):
                        g = b * CHUNKS + t
                        need(sp, S["s_psum"], 2 * g)
                        sp.dma_start(kT_now, view(kT_all, t * 512, 512)).then_inc(S["k_now"], 16)
                    i = t - 1
                    if live(i, CHUNKS):
                        g = b * CHUNKS + i
                        need(sp, S["o_psum"], g)
                        sp.dma_start(v_now, view(v_all, i * D, D)).then_inc(S["v_now"], 16)
                sp.wait_ge(S["kT_ready"], (b + 1) * CHUNKS)
                sp.wait_ge(S["v_ready"], (b + 1) * CHUNKS)
                sp.wait_ge(S["xT_kept"], (b + 1) * CHUNKS)
                sp.wait_ge(S["kv_psum"], (b + 1) * CHUNKS)
                steps(sp, CHUNKS, 1, 1, stage)
            sp.wait_ge(S["o_psum"], TILES)
            for t in range(TILES + 2):
                if t < TILES:
                    need(sp, S["attn_row"], 2 * (t - 3) - 1)
                    sp.dma_start(masked[:, (t % 4) * D:(t % 4 + 1) * D], x[t * P:(t + 1) * P, :]).then_inc(S["xr_in"][t % 4], 16)
                if t >= 2:
                    sp.wait_ge(S["attn_row"], 2 * (t - 1))
                    sp.dma_start(out[(t - 2) * P:(t - 1) * P, :], xy[:, (t - 2) * D:(t - 1) * D]).then_inc(S["attn_out"], 16)
            sp.wait_ge(S["attn_out"], 16 * TILES)
            for slot in range(4):
                sp.wait_ge(S["disp_out"][slot], 16 * TILES // 4)

            def load_sorted(t, slot):
                need(sp, S["ye_ready"], t - 3)
                need(sp, S["ids_ready"], t - 3)
                sp.dma_start(xs_buf[slot], sorted_d[bass.ds(t * P, P), :]).then_inc(S["xs_in"][slot], 16)
            for t in range(3):
                load_sorted(t, t)
            with sp.Fori(0, (SORTED - 3) // 4) as k:
                i = k * 4 + 3
                for u in range(4):
                    load_sorted(i + u, (3 + u) % 4)

        @block.gpsimd
        def _(gp):
            K = S["gp_const"]
            gp.memset(ident[:, :], 0.0).then_inc(K, 1)
            gp.memset(ones[:, :], 1.0).then_inc(K, 1)
            gp.memset(pad_row[:, :], 0.0).then_inc(S["pad_set"], 1)
            gp.iota(ini[:, :], [[P, CHUNKS]], base=0, channel_multiplier=1).then_inc(K, 1)
            gp.wait_ge(K, 3)
            gp.affine_select(out=ident[:, :], in_=ident[:, :], compare_op=ALU.not_equal, fill=1.0,
                             base=0, pattern=[[-1, P]], channel_multiplier=1).then_inc(K, 1)
            gp.affine_select(out=upper[:, :], in_=ones[:, :], compare_op=ALU.is_gt, fill=0.0,
                             base=0, pattern=[[1, P]], channel_multiplier=-1).then_inc(K, 1)
            gp.tensor_copy(pos0[:, :], ini[:, :]).then_inc(K, 1)
            gp.tensor_copy(ones_b[:, :], ones[:, :]).then_inc(K, 1)
            gp.wait_ge(S["pad_set"], 1)
            gp.memset(pad_row[:, D + 1:D + 2].bitcast(I32), NOBODY).then_inc(S["pad_set"], 1)
            gp.iota(tag[:, :].bitcast(I32).rearrange("p (t c) -> p t c", c=2)[:, :, 1:2], [[P, TILES], [0, 1]], base=0,
                    channel_multiplier=1).then_inc(K, 1)
            gp.memset(states[:, :], 0.0).then_inc(K, 1)
            gp.memset(qbd[:, :], 0.0).then_inc(K, 1)
            def split(src, dst, temp, low, n):
                done = 2 + 6 * n + (n > 0)
                cols = dst.shape[1]
                gp.wait_ge(S["bias_t"], done)
                for q in range(3):
                    gp.dma_start(temp[32 * q:32 * q + 1, 0:cols], src).then_inc(S["b_in"][0], 16)
                gp.wait_ge(S["b_in"][0], 48 * (n + 1))
                gp.tensor_copy(dst, temp[:, 0:cols]).then_inc(S["bias_t"], 1)
                gp.wait_ge(S["bias_t"], done + 1)
                gp.tensor_tensor(temp[:, 0:cols], temp[:, 0:cols], dst, ALU.subtract).then_inc(S["bias_t"], 1)
                gp.wait_ge(S["bias_t"], done + 2)
                gp.tensor_copy(low[:, 0:cols], temp[:, 0:cols]).then_inc(S["bias_t"], 1)
                gp.wait_ge(S["bias_t"], done + 3)
                gp.tensor_tensor(temp[:, 0:cols], temp[:, 0:cols], low[:, 0:cols], ALU.subtract).then_inc(S["bias_t"], 1)
                gp.wait_ge(S["bias_t"], done + 4)
                gp.tensor_copy(dst[32:33, :], low[32:33, 0:cols]).then_inc(S["bias_t"], 1)
                gp.wait_ge(S["bias_t"], done + 5)
                gp.tensor_copy(dst[64:65, :], temp[64:65, 0:cols]).then_inc(S["bias_t"], 1)

            gp.memset(small[:, 0:776], 0.0).then_inc(S["bias_t"], 1)
            gp.memset(bqkv_p[:, :], 0.0).then_inc(S["bias_t"], 1)
            split(bqkvu[0:1, 0:776], bqkv_p[:, 0:776], small[:, 0:776], small[:, 1024:1412].bitcast(BF16), 0)

            def state_for(b, c, par):
                g = b * CHUNKS + c
                need(gp, S["o_psum"], g - 1)
                need(gp, S["w_ready"], g - 1)
                t1 = states[:, CHUNKS * D:(CHUNKS + 1) * D]
                w = view(wstate, par * D, D)
                gp.tensor_tensor(w, t1, view(states, (c + 1) * D, D), ALU.subtract).then_inc(S["w_part"], 1)
                gp.tensor_tensor(wterm[:, par * D:(par + 1) * D], view(states, c * D, D), es_row[:, :], ALU.mult).then_inc(S["w_part"], 1)
                gp.wait_ge(S["w_part"], 2 * g + 2)
                gp.tensor_tensor(w, w, wterm[:, par * D:(par + 1) * D], ALU.add).then_inc(S["w_ready"], 1)

            gp.wait_ge(S["rows"], 3)
            gp.wait_ge(S["pad_out"], 16 * SORTED)
            for b in range(BATCH):
                need(gp, S["u_psum"], b * CHUNKS)
                with gp.Fori(0, CHUNKS // 2) as k:
                    for par in range(2):
                        i = k * 2 + par
                        gp.wait_ge(S["xT_ready"], b * CHUNKS + i + 1)
                        gp.tensor_copy(view(xT_all, i * D, D), xT_now[:, par * D:(par + 1) * D]).then_inc(S["xT_kept"], 1)
                gp.wait_ge(S["state_ready"], 2 * (b + 1) * CHUNKS)
                state_for(b, 0, 0)
                state_for(b, 1, 1)
                with gp.Fori(0, CHUNKS // 2 - 1) as k:
                    i = k * 2 + 2
                    state_for(b, i, 0)
                    state_for(b, i + 1, 1)

            gp.wait_ge(S["route_b"], 1)
            gp.wait_ge(S["pad_out"], 16 * SORTED)
            for t in range(TILES):
                gp.wait_ge(S["disp_in"][t % 4], 16 * (t // 4 + 1))
                gp.tensor_copy(disp[t % 4][:, D:D + 2].bitcast(U32), tag[:, 2 * t:2 * t + 2].bitcast(U32)).then_inc(S["disp_tag"], 1)
                gp.wait_ge(S["disp_tag"], t + 1)
                gp.indirect_dma_start(sorted_d[:, :], bass.IndirectOffsetOnAxis(ap=posi[:, t:t + 1], axis=0),
                                      disp[t % 4], None).then_inc(S["disp_out"][t % 4], 16)

            gp.wait_ge(S["attn_out"], 16 * TILES)
            gp.memset(xy[:, 6144:7168], 0.0).then_inc(S["bias_t"], 1)
            for n in range(EXPERTS):
                split(b1[n:n + 1, :], b1_p[:, n * FF:(n + 1) * FF], xy[:, 6144:7168], xy[:, 7168:7680].bitcast(BF16), 1 + n)
            for n in range(EXPERTS * D // FF):
                split(b2[0:1, n * FF:(n + 1) * FF], b2_p[:, n * FF:(n + 1) * FF], xy[:, 6144:7168],
                      xy[:, 7168:7680].bitcast(BF16), 1 + EXPERTS + n)

            gp.wait_ge(S["attn_out"], 16 * TILES)

            last_row = gp.to_reg(TILES * P - 1)

            def combine(t, slot):
                gp.wait_ge(S["ye_ready"], t + 1)
                gp.wait_ge(S["ids_ready"], t + 1)
                gp.indirect_dma_start(out[:, :], bass.IndirectOffsetOnAxis(ap=ids[:, slot:slot + 1], axis=0),
                                      moe_y[slot], None, bounds_check=last_row, oob_is_err=False,
                                      compute_op=ALU.add).then_inc(S["ye_out"][slot], 16)
            for t in range(SORTED):
                combine(t, t % 4)
            for slot in range(4):
                gp.wait_ge(S["ye_out"][slot], 16 * len(range(slot, SORTED, 4)))

        @block.scalar
        def _(act):
            C = S["const_in"]
            act.dma_start(theta_row[:, :], theta[0:1, :].broadcast_to([P, D])).then_inc(C, 16)
            act.dma_start(slope_bc[:, :], slope[0:1, :].broadcast_to([P, HEADS])).then_inc(C, 16)
            act.dma_start(wproj[:, :], wqkvu).then_inc(C, 16)
            act.dma_start(wo_sb[:, :], wout).then_inc(C, 16)
            act.dma_start(bu_col[:, :], bu_cols).then_inc(C, 16)
            act.dma_start(bout_row[:, :], bout[0:1, :].broadcast_to([P, D])).then_inc(C, 16)
            act.wait_ge(C, 96)
            act.activation(es[:, :], slope_bc[:, :], ACT.Exp).then_inc(S["rows"], 1)
            act.wait_ge(S["stat_a"], TILES + 1)
            act.activation(rstd[:, :], mv[:, 1::2], ACT.Sqrt).then_inc(S["stat_b"], 1)
            for q in range(4):
                act.wait_ge(S["tab"], 7 * q + 7)
                r = trig[:, 0:1024]
                a = trig[:, 1024:2048]
                act.wait_ge(S["stat_c"], 3 * q + 1)
                act.activation(sin_all[:, q * 1024:(q + 1) * 1024], r, ACT.Sin).then_inc(S["stat_c"], 1)
                act.activation(a, r, ACT.Abs).then_inc(S["stat_c"], 1)
                act.wait_ge(S["stat_c"], 3 * q + 3)
                act.activation(cos_all[:, q * 1024:(q + 1) * 1024], a, ACT.Sin, scale=-1.0,
                               bias=halfpi[:, 0:1]).then_inc(S["stat_c"], 1)

            for b in range(BATCH):
                def step_a(t, par, b=b):
                    if live(t, CHUNKS):
                        g = b * CHUNKS + t
                        act.wait_ge(S["xT_psum"], g + 1)
                        need(act, S["kv_psum"], g - 1)
                        need(act, S["xT_kept"], g - 1)
                        act.activation(xT_now[:, par * D:(par + 1) * D], ps[0][:, 0:D], ACT.Copy).then_inc(S["xT_ready"], 1)
                    i = t - 1
                    if live(i, CHUNKS):
                        g = b * CHUNKS + i
                        q = 1 - par
                        act.wait_ge(S["kv_psum"], g + 1)
                        need(act, S["rope_k"], 2 * (g - 1))
                        act.activation(view(act_k, q * D, D), ps[1][:, 0:D], ACT.Silu).then_inc(S["k_act"], 1)
                        act.activation(view(logits, g * EXPERTS, EXPERTS), ps[1][:, D:D + EXPERTS],
                                       ACT.Copy).then_inc(S["lg_ready"], 1)
                        act.activation(view(v_all, i * D, D), ps[2][:, 0:D], ACT.Copy).then_inc(S["v_ready"], 1)
                if b:
                    act.wait_ge(S["z_ready"], 2 * b * CHUNKS)
                    act.wait_ge(S["o_psum"], b * CHUNKS)
                    act.wait_ge(S["rope_q"], 2 * b * CHUNKS)
                steps(act, CHUNKS, 0, 1, step_a)

                def step_b(t, par, b=b):
                    i = t - 1
                    if live(i, CHUNKS):
                        g = b * CHUNKS + i
                        q = 1 - par
                        act.wait_ge(S["qT_psum"], g + 1)
                        need(act, S["o_psum"], g - 1)
                        act.activation(view(qT, q * 512, 512), ps[0][:, :], ACT.Copy).then_inc(S["q_moved"], 1)
                        need(act, S["s_psum"], 2 * g)
                        for h in range(2):
                            act.activation(qbd[64 * h:64 * h + 64, 0:1024].rearrange("p (a h n) -> p a h n", a=4, h=2)[:, :, h, :],
                                           ps[0][64 * h:64 * h + 64, :].rearrange("p (a n) -> p a n", a=4),
                                           ACT.Copy).then_inc(S["q_moved"], 1)
                    if live(t, CHUNKS):
                        g = b * CHUNKS + t
                        act.wait_ge(S["q_psum"], g + 1)
                        need(act, S["rope_q"], 2 * (g - 1))
                        act.activation(view(act_k, par * D, D), ps[1 + par][:, 0:D], ACT.Silu).then_inc(S["q_act"], 1)
                    i = t - 2
                    if live(i, CHUNKS):
                        g = b * CHUNKS + i
                        act.wait_ge(S["o_psum"], g + 1)
                        need(act, S["z_ready"], 2 * g)
                        act.activation(oT[:, :], ps[5][:, 0:D], ACT.Copy).then_inc(S["o_moved"], 1)
                        need(act, S["y_psum"], g)
                        act.activation(osq[:, :], ps[5][:, 0:D], ACT.Square).then_inc(S["o_moved"], 1)
                act.wait_ge(S["rope_k"], 2 * (b + 1) * CHUNKS)
                steps(act, CHUNKS, 0, 2, step_b)

            act.wait_ge(S["route_a"], 8)
            act.activation(small[:, 0:TILES], ms[:, :], ACT.Sqrt).then_inc(S["route_act"], 1)
            act.activation(small[:, 320:576], small[:, 64:320], ACT.Exp).then_inc(S["route_act"], 1)
            for q in range(2):
                act.wait_ge(S["xn_out"][q], 8 * TILES)
            for t in range(TILES):
                if t >= 4:
                    act.wait_ge(S["disp_out"][t % 4], 16 * (t // 4))
                act.dma_start(disp[t % 4][:, 0:D], xn_d[t * P:(t + 1) * P, :]).then_inc(S["disp_in"][t % 4], 16)
            act.wait_ge(S["attn_row"], 2 * TILES)
            for e in range(EXPERTS):
                act.dma_start(region[:, e * WSIZE:e * WSIZE + KC * FF], w1[:, e * KC * FF:(e + 1) * KC * FF]).then_inc(S["wt_in"], 16)
                act.dma_start(region[:, e * WSIZE + KC * FF:(e + 1) * WSIZE], w2[:, e * FC * D:(e + 1) * FC * D]).then_inc(S["wt_in"], 16)

            act.wait_ge(S["attn_out"], 16 * TILES)

            def step(t, m):
                if live(t, SORTED):
                    act.wait_ge(S["xt_psum"], t + 1)
                    need(act, S["h_psum"], 2 * (t - 1))
                    act.activation(moe_xT[m % 2], ps[0][:, 0:D], ACT.Copy).then_inc(S["xt_ready"], 1)
                i = t - 1
                if live(i, SORTED):
                    for n in range(2):
                        act.wait_ge(S["h_psum"], 2 * i + n + 1)
                        need(act, S["hT_psum"], 2 * i)
                        act.activation(moe_h[:, n * 512:(n + 1) * 512], ps[1 + n][:, :], ACT.Relu).then_inc(S["h_ready"], 1)
                i = t - 2
                if live(i, SORTED):
                    k = (m - 2) % 4
                    act.wait_ge(S["ye_psum"], i + 1)
                    need(act, S["ye_out"][k], 4 * (i - k))
                    act.activation(moe_y[k], ps[5][:, 0:D], ACT.Copy, scale=xs_buf[k][:, D:D + 1]).then_inc(S["ye_ready"], 1)
            for t in range(7):
                step(t, t % 4)
            with act.Fori(0, (SORTED - 7) // 4) as k:
                i = k * 4 + 7
                for u in range(4):
                    step(i + u, (7 + u) % 4)
            for t in range(SORTED, SORTED + 2):
                step(t, t % 4)

        @block.vector
        def _(dve):
            v = nc.vector
            for t in range(TILES):
                dve.wait_ge(S["x_in"][t // 4], 16)
                v.bn_stats(stats[:, 6 * t:6 * t + 6], xy[:, t * D:(t + 1) * D]).then_inc(S["ln_part"], 1)
            for t in range(TILES):
                dve.wait_ge(S["ln_part"], t + 1)
                v.bn_aggr(mv[:, 2 * t:2 * t + 2], stats[:, 6 * t:6 * t + 6]).then_inc(S["stat_a"], 1)
            dve.wait_ge(S["stat_a"], TILES)
            v.tensor_scalar(mv[:, 1::2], mv[:, 1::2], LN_EPS, None, ALU.add).then_inc(S["stat_a"], 1)
            v.memset(halfpi[:, :], float(np.pi / 2)).then_inc(S["stat_c"], 1)
            dve.wait_ge(S["stat_b"], 1)
            v.reciprocal(rstd[:, :], rstd[:, :]).then_inc(S["stat_b"], 1)
            dve.wait_ge(S["const_in"], 96)
            dve.wait_ge(S["gp_const"], 10)
            r = trig[:, 0:1024]
            turns = trig[:, 2048:3072]
            T = S["tab"]
            for q in range(4):
                if q:
                    dve.wait_ge(S["stat_c"], 3 * q + 1)
                for k in range(4):
                    c = 4 * q + k
                    ins = v.tensor_scalar(r[:, k * D:(k + 1) * D], theta_row[:, :], pos0[:, c:c + 1], None, ALU.mult)
                ins.then_inc(T, 1)
                dve.wait_ge(T, 7 * q + 1)
                v.tensor_scalar(turns, r, float(1 / (2 * np.pi)), ROUND, ALU.mult, ALU.add).then_inc(T, 1)
                dve.wait_ge(T, 7 * q + 2)
                v.tensor_scalar(turns, turns, ROUND, None, ALU.subtract).then_inc(T, 1)
                for n, part_of in enumerate((TWO_PI_A, TWO_PI_B, TWO_PI_C)):
                    dve.wait_ge(T, 7 * q + 3 + n)
                    v.scalar_tensor_tensor(r, turns, -part_of, r, ALU.mult, ALU.add).then_inc(T, 1)
                dve.wait_ge(T, 7 * q + 6)
                v.tensor_scalar(r, r, PI_IN, -PI_IN, ALU.min, ALU.max).then_inc(T, 1)
            dve.wait_ge(S["rows"], 1)
            dve.wait_ge(S["bias_t"], 8)
            v.tensor_tensor(small[:, 0:P], upper[:, :], ident[:, :], ALU.add).then_inc(S["mask_part"], 1)
            v.tensor_scalar(slope_bc[:, :], es[:, :], -1.0, None, ALU.add).then_inc(S["mask_part"], 1)
            dve.wait_ge(S["mask_part"], 2)
            for h in range(HEADS):
                ins = v.tensor_scalar(mask[:, h * P:(h + 1) * P], small[:, 0:P], slope_bc[:, h:h + 1], 1.0, ALU.mult, ALU.add)
            ins.then_inc(S["rows"], 1)
            v.tensor_copy(es_row[:, :].rearrange("p (h d) -> p h d", d=HD),
                          es[:, :].rearrange("p (h a) -> p h a", a=1).broadcast_to([P, HEADS, HD])).then_inc(S["rows"], 1)

            def rope(src, dst, c, done):
                d4 = dst.rearrange("p (h s d) -> p h s d", h=HEADS, s=2)
                s3 = src.rearrange("p (h d) -> p h d", d=HD)
                for n, table in enumerate((cos_all, sin_all)):
                    v.tensor_tensor(d4[:, :, n, :], s3, view(table, c * D, D).rearrange("p (h d) -> p h d", d=HD),
                                    ALU.mult).then_inc(done, 1)

            dve.wait_ge(S["stat_c"], 13)
            dve.wait_ge(S["stat_b"], 2)
            dve.wait_ge(S["rows"], 3)
            for b in range(BATCH):
                def step_a(t, par, b=b):
                    if live(t + 1, CHUNKS):
                        g = b * CHUNKS + t + 1
                        need(dve, S["xT_psum"], g - 1)
                        need(dve, S["xn_out"][1 - par], 8 * (g - (1 - par)))
                        v.tensor_scalar(view(xn, (1 - par) * D, D), view(xy, g * D, D),
                                        view(mv, 2 * g, 1), view(rstd, g, 1),
                                        ALU.subtract, ALU.mult).then_inc(S["xn_ready"], 1)
                    i = t - 1
                    if live(i, CHUNKS):
                        g = b * CHUNKS + i
                        q = 1 - par
                        dve.wait_ge(S["k_act"], g + 1)
                        need(dve, S["state_psum"], g - 1)
                        rope(view(act_k, q * D, D), view(rot, q * 512, 512), i, S["rope_k"])
                    i = t - 2
                    if live(i, CHUNKS):
                        g = b * CHUNKS + i
                        dve.wait_ge(S["kT_psum"], g + 1)
                        v.tensor_copy(view(kT_all, i * 512, 512), ps[3][:, :]).then_inc(S["kT_ready"], 1)
                        dve.wait_ge(S["state_psum"], g + 1)
                        need(dve, S["state_ready"], 2 * g)
                        for h in range(2):
                            lo, hi = 64 * h, 64 * h + 64
                            one = ps[4][lo:hi, :].rearrange("p (g a c) -> p g a c", g=2, a=4)[:, :, 0:4:3, 32 * h:32 * h + 32]
                            before = states[lo:hi, bass.ds(i * D, D)].rearrange("p (g a c) -> p g a c", g=2, a=2)[:, :, :, 32 * h:32 * h + 32]
                            after = states[lo:hi, bass.ds((i + 1) * D, D)].rearrange("p (g a c) -> p g a c", g=2, a=2)[:, :, :, 32 * h:32 * h + 32]
                            v.tensor_tensor(after, one, before, ALU.add).then_inc(S["state_ready"], 1)
                if b:
                    dve.wait_ge(S["w_ready"], b * CHUNKS)
                    dve.wait_ge(S["qT_psum"], b * CHUNKS)
                    dve.wait_ge(S["s_psum"], 2 * b * CHUNKS)
                steps(dve, CHUNKS, 1, 2, step_a)

                def step_b(t, par, b=b):
                    if live(t, CHUNKS):
                        g = b * CHUNKS + t
                        dve.wait_ge(S["q_act"], g + 1)
                        need(dve, S["qT_psum"], g - 1)
                        rope(view(act_k, par * D, D), view(rot, par * 512, 512), t, S["rope_q"])
                    i = t - 1
                    if live(i, CHUNKS):
                        g = b * CHUNKS + i
                        q = 1 - par
                        need(dve, S["o_psum"], g - 1)
                        for n in range(2):
                            dve.wait_ge(S["s_psum"], 2 * g + n + 1)
                            v.tensor_tensor(view(masked, q * 1024 + n * 512, 512), ps[3 + n][:, :],
                                            mask[:, n * 512:(n + 1) * 512], ALU.mult).then_inc(S["s_masked"], 1)
                    i = t - 3
                    if live(i, CHUNKS):
                        g = b * CHUNKS + i
                        dve.wait_ge(S["y_psum"], g + 1)
                        v.tensor_copy(view(xy, g * D, D), ps[7][:, 0:D]).then_inc(S["y_moved"], 1)
                        v.tensor_scalar(view(ms, g, 1), ps[7][:, D:D + 1], 1.0 / D, RMS_EPS,
                                        ALU.mult, ALU.add).then_inc(S["y_moved"], 1)
                    i = t - 2
                    if live(i, CHUNKS):
                        g = b * CHUNKS + i
                        dve.wait_ge(S["o_moved"], 2 * g + 1)
                        dve.wait_ge(S["u_psum"], g + 1)
                        need(dve, S["y_psum"], g)
                        for n in range(KC):
                            v.scalar_tensor_tensor(zT[:, n * P:(n + 1) * P], ps[6][:, n * P:(n + 1) * P],
                                                   bu_col[:, n:n + 1], oT[:, n * P:(n + 1) * P],
                                                   ALU.add, ALU.mult).then_inc(S["z_ready"], 1)
                dve.wait_ge(S["state_psum"], (b + 1) * CHUNKS)
                steps(dve, CHUNKS, 0, 3, step_b)

            A = S["route_a"]
            L = logits[:, :].rearrange("p (t e) -> p t e", e=EXPERTS)
            mx = small[:, 32:64]

            def per_tile(ap):
                return ap.rearrange("p (t a) -> p t a", a=1).broadcast_to([P, TILES, EXPERTS])

            less = small[:, 64:320].rearrange("p (t e) -> p t e", e=EXPERTS)
            ex = small[:, 320:576].rearrange("p (t e) -> p t e", e=EXPERTS)
            pick = small[:, 576:832].rearrange("p (t e) -> p t e", e=EXPERTS)
            rank = small[:, 832:840]
            dve.wait_ge(S["lg_ready"], TILES)
            dve.wait_ge(S["y_moved"], 2 * TILES)
            for q in range(2):
                dve.wait_ge(S["xn_out"][q], 8 * TILES)
            v.reduce_max(mx, L, AX.X).then_inc(A, 1)
            for e in range(EXPERTS):
                ins = v.memset(rank[:, e:e + 1], float(EXPERTS - e))
            ins.then_inc(A, 1)
            dve.wait_ge(A, 2)
            v.tensor_tensor(less, L, per_tile(mx), ALU.subtract).then_inc(A, 1)
            v.tensor_tensor(pick, L, per_tile(mx), ALU.is_equal).then_inc(A, 1)
            dve.wait_ge(A, 4)
            v.tensor_tensor(pick, pick, rank.rearrange("p (a e) -> p a e", a=1).broadcast_to([P, TILES, EXPERTS]),
                            ALU.mult).then_inc(A, 1)
            dve.wait_ge(A, 5)
            v.reduce_max(small[:, 840:872], pick, AX.X).then_inc(A, 1)
            dve.wait_ge(A, 6)
            onehot = small[:, 872:1128]
            v.tensor_tensor(onehot.rearrange("p (e t) -> p t e", e=EXPERTS), pick, per_tile(small[:, 840:872]),
                            ALU.is_equal).then_inc(A, 1)
            v.memset(small[:, 1128:1160], 1.0).then_inc(A, 1)
            dve.wait_ge(S["route_act"], 2)
            v.reduce_sum(small[:, 840:872], ex, AX.X).then_inc(A, 1)
            dve.wait_ge(A, 9)
            v.reciprocal(tag[:, 0::2], small[:, 840:872]).then_inc(A, 1)
            v.reciprocal(rstd[:, :], small[:, 0:TILES]).then_inc(A, 1)
            dve.wait_ge(S["route_pe"], 2)
            incl = small[:, 576:832]
            for e in range(EXPERTS):
                v.tensor_tensor_scan(incl[:, e * TILES:(e + 1) * TILES], small[:, 1128:1160],
                                     ps[4][:, e * TILES:(e + 1) * TILES], 0.0, ALU.mult, ALU.add).then_inc(A, 1)
            n = 11 + EXPERTS
            dve.wait_ge(A, n)
            i3 = incl.rearrange("p (e t) -> p e t", e=EXPERTS)
            padded_i = experts_i[:, 0:EXPERTS]
            v.tensor_scalar(padded_i, i3[:, :, TILES - 1], float(P - 1), None, ALU.add).then_inc(A, 1)
            dve.wait_ge(A, n + 1)
            v.tensor_scalar(padded_i, padded_i, P.bit_length() - 1, P.bit_length() - 1, ALU.logical_shift_right,
                            ALU.logical_shift_left).then_inc(A, 1)
            dve.wait_ge(A, n + 2)
            padded = small[:, 1168:1176]
            ends = small[:, 1176:1184]
            v.tensor_copy(padded, padded_i).then_inc(A, 1)
            dve.wait_ge(A, n + 3)
            v.tensor_tensor_scan(ends, small[:, 1128:1136], padded, 0.0, ALU.mult, ALU.add).then_inc(A, 1)
            v.tensor_tensor(incl, incl, ps[4][:, 0:256], ALU.subtract).then_inc(A, 1)
            dve.wait_ge(A, n + 5)
            v.tensor_tensor(padded, ends, padded, ALU.subtract).then_inc(A, 1)
            v.tensor_tensor(incl, incl, ps[3][:, 0:256], ALU.add).then_inc(A, 1)
            dve.wait_ge(A, n + 7)
            v.tensor_tensor(i3, i3, padded.rearrange("p (e a) -> p e a", a=1).broadcast_to([P, EXPERTS, TILES]),
                            ALU.add).then_inc(A, 1)
            dve.wait_ge(A, n + 8)
            v.tensor_tensor(incl, incl, onehot, ALU.mult).then_inc(A, 1)
            dve.wait_ge(A, n + 9)
            v.reduce_sum(small[:, 840:872], incl.rearrange("p (e t) -> p t e", e=EXPERTS), AX.X).then_inc(A, 1)
            dve.wait_ge(A, n + 10)
            v.tensor_copy(posi[:, :], small[:, 840:872]).then_inc(S["route_b"], 1)
            over = small[:, 1184:1184 + SORTED * EXPERTS].rearrange("p (j e) -> p j e", e=EXPERTS)
            for j in range(SORTED):
                ins = v.tensor_scalar(over[:, j, :], ends, float(j * P), None, ALU.is_le)
            ins.then_inc(A, 1)
            dve.wait_ge(A, n + 11)
            v.reduce_sum(small[:, 576:576 + SORTED], over, AX.X).then_inc(A, 1)
            dve.wait_ge(A, n + 12)
            v.tensor_scalar(experts_i[:, :], small[:, 576:576 + SORTED], float(EXPERTS - 1), None,
                            ALU.min).then_inc(S["route_b"], 1)

            dve.wait_ge(A, 11)
            for t in range(TILES):
                res = masked[:, (t % 4) * D:(t % 4 + 1) * D]
                row = xy[:, t * D:(t + 1) * D]
                dve.wait_ge(S["xr_in"][t % 4], 16 * (t // 4 + 1))
                v.scalar_tensor_tensor(row, row, rstd[:, t:t + 1], res, ALU.mult, ALU.add).then_inc(S["attn_row"], 1)
                dve.wait_ge(S["attn_row"], 2 * t + 1)
                v.tensor_tensor(row, row, bout_row[:, :], ALU.add).then_inc(S["attn_row"], 1)

            dve.wait_ge(S["attn_out"], 16 * TILES)

            def step(t, m):
                i = t - 2
                if live(t, SORTED):
                    dve.wait_ge(S["xs_in"][m], 4 * (t - m) + 16)
                    need(dve, S["ye_out"][m], 4 * (t - m))
                    v.tensor_copy(ids[:, m:m + 1], xs_buf[m][:, D + 1:D + 2].bitcast(U32)).then_inc(S["ids_ready"], 1)
                if live(i, SORTED):
                    for n in range(2):
                        dve.wait_ge(S["hT_psum"], 2 * i + n + 1)
                        need(dve, S["ye_psum"], i)
                        v.tensor_copy(moe_hT[:, n * 512:(n + 1) * 512], ps[3 + n][:, :]).then_inc(S["hT_ready"], 1)
            for t in range(3):
                step(t, t)
            with dve.Fori(0, (SORTED - 3) // 4) as k:
                i = k * 4 + 3
                for u in range(4):
                    step(i + u, (3 + u) % 4)
            for t in range(SORTED, SORTED + 2):
                step(t, t % 4)

        @block.tensor
        def _(pe):
            mm = nc.tensor.matmul
            pe.wait_ge(S["gp_const"], 10)
            pe.wait_ge(S["const_in"], 96)
            pe.wait_ge(S["bias_t"], 8)
            pe.wait_ge(S["rows"], 3)

            def wp(k, lo, hi):
                return wproj[:, k * 1032 + lo:k * 1032 + hi]

            for b in range(BATCH):
                def step_a(t, par, b=b):
                    if live(t, CHUNKS):
                        g = b * CHUNKS + t
                        pe.wait_ge(S["xn_ready"], g + 1)
                        need(pe, S["xT_ready"], g)
                        for k in range(KC):
                            ins = nc.tensor.transpose(ps[0][:, k * P:(k + 1) * P], view(xn, par * D + k * P, P), ident[:, :])
                        ins.then_inc(S["xT_psum"], 1)
                    i = t - 1
                    if live(i, CHUNKS):
                        g = b * CHUNKS + i
                        pe.wait_ge(S["xT_ready"], g + 1)
                        need(pe, S["k_act"], g)
                        need(pe, S["v_ready"], g)
                        need(pe, S["lg_ready"], g)
                        mm(ps[1][:, 0:264], ones_b[:, :], bqkv_p[:, 0:264], start=True, stop=False)
                        mm(ps[2][:, 0:D], ones_b[:, :], bqkv_p[:, 264:520], start=True, stop=False)
                        for k in range(KC):
                            xk = xT_now[:, (1 - par) * D + k * P:(1 - par) * D + (k + 1) * P]
                            mm(ps[1][:, 0:264], xk, wp(k, 0, 264), start=False, stop=k == KC - 1)
                            ins = mm(ps[2][:, 0:D], xk, wp(k, 264, 520), start=False, stop=k == KC - 1)
                        ins.then_inc(S["kv_psum"], 1)
                    i = t - 2
                    if live(i, CHUNKS):
                        g = b * CHUNKS + i
                        pe.wait_ge(S["rope_k"], 2 * g + 2)
                        need(pe, S["kT_ready"], g)
                        for a in range(4):
                            ins = nc.tensor.transpose(ps[3][:, a * P:(a + 1) * P], view(rot, par * 512 + a * P, P), ident[:, :])
                        ins.then_inc(S["kT_psum"], 1)
                        pe.wait_ge(S["v_ready"], g + 1)
                        need(pe, S["state_ready"], 2 * g)
                        for a in range(4):
                            ins = mm(ps[4][:, a * P:(a + 1) * P], view(rot, par * 512 + a * P, P),
                                     view(v_all, i * D + (a // 2) * P, P), start=True, stop=True)
                        ins.then_inc(S["state_psum"], 1)
                if b:
                    pe.wait_ge(S["q_moved"], 3 * b * CHUNKS)
                    pe.wait_ge(S["q_act"], b * CHUNKS)
                    pe.wait_ge(S["s_masked"], 2 * b * CHUNKS)
                steps(pe, CHUNKS, 0, 2, step_a)

                def step_b(t, par, b=b):
                    i = t - 1
                    q = 1 - par
                    if live(i, CHUNKS):
                        g = b * CHUNKS + i
                        pe.wait_ge(S["rope_q"], 2 * g + 2)
                        need(pe, S["q_moved"], 3 * g)
                        for a in range(4):
                            ins = nc.tensor.transpose(ps[0][:, a * P:(a + 1) * P], view(rot, q * 512 + a * P, P), ident[:, :])
                        ins.then_inc(S["qT_psum"], 1)
                    if live(t, CHUNKS):
                        g = b * CHUNKS + t
                        need(pe, S["q_act"], g - 1)
                        pe.wait_ge(S["x_now"][par], 8 * (g - par) + 16)
                        mm(ps[1 + par][:, 0:D], ones_b[:, :], bqkv_p[:, 520:776], start=True, stop=False)
                        for k in range(KC):
                            ins = mm(ps[1 + par][:, 0:D], xT_now[:, par * D + k * P:par * D + (k + 1) * P], wp(k, 520, 776),
                                     start=False, stop=k == KC - 1)
                        ins.then_inc(S["q_psum"], 1)
                    if live(i, CHUNKS):
                        g = b * CHUNKS + i
                        pe.wait_ge(S["q_moved"], 3 * g + 3)
                        pe.wait_ge(S["k_now"], 16 * g + 16)
                        for n in range(2):
                            need(pe, S["s_masked"], 2 * g - 1 + n)
                            for a in range(2):
                                pair = 2 * n + a
                                ins = mm(ps[3 + n][:, a * D:(a + 1) * D], kT_now[:, pair * P:(pair + 1) * P],
                                         qbd[:, pair * D:(pair + 1) * D], start=True, stop=True)
                            ins.then_inc(S["s_psum"], 1)
                    i = t - 3
                    if live(i, CHUNKS):
                        g = b * CHUNKS + i
                        pe.wait_ge(S["z_ready"], 2 * g + 2)
                        pe.wait_ge(S["o_moved"], 2 * g + 2)
                        need(pe, S["y_moved"], 2 * g)
                        for k in range(KC):
                            mm(ps[7][:, 0:D], zT[:, k * P:(k + 1) * P], wo_sb[:, k * D:(k + 1) * D],
                               start=k == 0, stop=k == KC - 1)
                        for k in range(KC):
                            ins = mm(ps[7][:, D:D + 1], osq[:, k * P:(k + 1) * P], ones[:, 0:1],
                                     start=k == 0, stop=k == KC - 1)
                        ins.then_inc(S["y_psum"], 1)
                    i = t - 2
                    if live(i, CHUNKS):
                        g = b * CHUNKS + i
                        need(pe, S["z_ready"], 2 * g)
                        for n in range(KC):
                            for k in range(KC):
                                ins = mm(ps[6][:, n * P:(n + 1) * P], wp(k, 776 + n * P, 776 + (n + 1) * P),
                                         view(xT_all, i * D + k * P, P), start=k == 0, stop=k == KC - 1)
                        ins.then_inc(S["u_psum"], 1)
                        pe.wait_ge(S["v_now"], 16 * g + 16)
                        pe.wait_ge(S["w_ready"], g + 1)
                        need(pe, S["o_moved"], 2 * g)
                        pe.wait_ge(S["s_masked"], 2 * g + 2)
                        for n in range(2):
                            for a in range(2):
                                pair = 2 * n + a
                                mm(ps[5][64 * a:64 * a + 64, n * P:(n + 1) * P], view(wstate, par * D + pair * 64, 64),
                                   view(qT, par * 512 + pair * P, P), start=True, stop=False, skip_group_check=True)
                            for hh in range(4):
                                h = 4 * n + hh
                                ins = mm(ps[5][32 * hh:32 * hh + 32, n * P:(n + 1) * P], v_now[:, h * HD:(h + 1) * HD],
                                         view(masked, par * 1024 + h * P, P), start=False, stop=True,
                                         skip_group_check=True)
                        ins.then_inc(S["o_psum"], 1)
                pe.wait_ge(S["xT_ready"], (b + 1) * CHUNKS)
                pe.wait_ge(S["k_act"], (b + 1) * CHUNKS)
                pe.wait_ge(S["v_ready"], (b + 1) * CHUNKS)
                pe.wait_ge(S["lg_ready"], (b + 1) * CHUNKS)
                pe.wait_ge(S["kT_ready"], (b + 1) * CHUNKS)
                pe.wait_ge(S["state_ready"], 2 * (b + 1) * CHUNKS)
                steps(pe, CHUNKS, 0, 3, step_b)

            pe.wait_ge(S["route_a"], 7)
            mm(ps[3][:, 0:256], upper[:, :], small[:, 872:1128], start=True, stop=True).then_inc(S["route_pe"], 1)
            mm(ps[4][:, 0:256], ones[:, :], small[:, 872:1128], start=True, stop=True).then_inc(S["route_pe"], 1)

            pe.wait_ge(S["route_b"], 2)
            pe.wait_ge(S["attn_out"], 16 * TILES)
            pe.wait_ge(S["bias_t"], 3 + 6 * (1 + EXPERTS + EXPERTS * D // FF))
            pe.wait_ge(S["wt_in"], 32 * EXPERTS)

            def step(t, m):
                if live(t, SORTED):
                    pe.wait_ge(S["xs_in"][m], 4 * (t - m) + 16)
                    need(pe, S["xt_ready"], t)
                    for k in range(KC):
                        ins = nc.tensor.transpose(ps[0][:, k * P:(k + 1) * P], xs_buf[m][:, k * P:(k + 1) * P], ident[:, :])
                    ins.then_inc(S["xt_psum"], 1)
                i = t - 2
                if live(i, SORTED):
                    for n in range(2):
                        pe.wait_ge(S["h_ready"], 2 * i + n + 1)
                        need(pe, S["hT_ready"], 2 * i - 1 + n)
                        for k in range(4):
                            ins = nc.tensor.transpose(ps[3 + n][:, k * P:(k + 1) * P],
                                                      moe_h[:, (4 * n + k) * P:(4 * n + k + 1) * P], ident[:, :])
                        ins.then_inc(S["hT_psum"], 1)
                i = t - 1
                if live(i, SORTED):
                    e = nc.tensor.value_load(experts_i[0:1, bass.ds(i, 1)], min_val=0, max_val=EXPERTS - 1)
                    pe.wait_ge(S["xt_ready"], i + 1)
                    for n in range(2):
                        need(pe, S["h_ready"], 2 * i - 1 + n)
                        mm(ps[1 + n][:, :], ones_b[:, :], view(b1_p, e * FF + n * 512, 512), start=True, stop=False)
                        for k in range(KC):
                            ins = mm(ps[1 + n][:, :], moe_xT[(m - 1) % 2][:, k * P:(k + 1) * P],
                                     view(region, e * WSIZE + k * FF + n * 512, 512), start=False, stop=k == KC - 1)
                        ins.then_inc(S["h_psum"], 1)
                i = t - 2
                if live(i, SORTED):
                    e = nc.tensor.value_load(experts_i[0:1, bass.ds(i, 1)], min_val=0, max_val=EXPERTS - 1)
                    need(pe, S["ye_ready"], i)
                    mm(ps[5][:, 0:D], ones_b[:, :], view(b2_p, e * D, D), start=True, stop=False)
                    for f in range(FC):
                        if f % 4 == 0:
                            pe.wait_ge(S["hT_ready"], 2 * i + f // 4 + 1)
                        ins = mm(ps[5][:, 0:D], moe_hT[:, f * P:(f + 1) * P],
                                 view(region, e * WSIZE + KC * FF + f * D, D), start=False, stop=f == FC - 1)
                    ins.then_inc(S["ye_psum"], 1)
            for t in range(3):
                step(t, t)
            with pe.Fori(0, (SORTED - 3) // 4) as k:
                i = k * 4 + 3
                for u in range(4):
                    step(i + u, (3 + u) % 4)
            for t in range(SORTED, SORTED + 2):
                step(t, t % 4)


def kernel(**inputs):
    import concourse.bacc as bacc
    from concourse.bass_utils import run_bass_kernel_spmd

    g = {n: np.asarray(a) for n, a in inputs.items()}
    wt = g["L0_attn_qkvu_w"].T
    q, k, v, u = (wt[:, n * D:(n + 1) * D] for n in range(4))
    proj = np.concatenate([k, g["L0_ffn_w_router"], v, q, u], axis=1)
    bq, bk, bv, bu = (g["L0_attn_qkvu_b"][n * D:(n + 1) * D] for n in range(4))
    bias = np.concatenate([bk, np.zeros(EXPERTS, np.float32), bv, bq, bu])[None]

    def rows(w, chunks):
        return np.ascontiguousarray(w.reshape(chunks, P, -1).transpose(1, 0, 2).reshape(P, -1))

    w1 = g["L0_ffn_w1"].reshape(EXPERTS, KC, P, FF).transpose(2, 0, 1, 3).reshape(P, -1)
    w2 = g["L0_ffn_w2"].reshape(EXPERTS, FC, P, D).transpose(2, 0, 1, 3).reshape(P, -1)
    arrays = {
        "x": g["L0_attn_x"].reshape(-1, D), "slope": g["L0_attn_slope_rate"].reshape(1, HEADS),
        "wqkvu": rows(proj, KC), "bqkvu": bias, "wout": rows(g["L0_attn_out_w"].T, KC),
        "bout": g["L0_attn_out_b"][None], "theta": g["L0_attn_theta"].reshape(1, D),
        "bu_cols": bu.reshape(KC, P).T, "w1": w1, "b1": g["L0_ffn_b1"], "w2": w2,
        "b2": g["L0_ffn_b2"].reshape(1, -1),
    }
    arrays = {n: np.ascontiguousarray(a) for n, a in arrays.items()}
    nc = bacc.Bacc("TRN2", target_bir_lowering=False, num_devices=1)
    args = [nc.dram_tensor(n, a.shape, mybir.dt.from_np(a.dtype), kind="ExternalInput").ap() for n, a in arrays.items()]
    out = nc.dram_tensor("out", (TILES * P, D), F32, kind="ExternalOutput").ap()
    xn_d = nc.dram_tensor("xn_rows", (TILES * P, D), F32).ap()
    sorted_d = nc.dram_tensor("sorted_rows", (SORTED * P, ROW), F32).ap()
    build(nc, *args, out, xn_d, sorted_d)
    r = run_bass_kernel_spmd(nc, [arrays], core_ids=[0])
    return r.results[0]["out"].reshape(BATCH, SEQ, D)
```

```python
from contextlib import ExitStack

import numpy as np
import concourse.bass as bass
from concourse import mybir

F32 = mybir.dt.float32
F16 = mybir.dt.float16
BF16 = mybir.dt.bfloat16
I32 = mybir.dt.int32
U32 = mybir.dt.uint32
ALU = mybir.AluOpType
ACT = mybir.ActivationFunctionType
AX = mybir.AxisListType

P = 128
BATCH, SEQ, D = 2, 2048, 256
HEADS, HD = 8, 32
EXPERTS, FF = 8, 1024
KC = D // P
CHUNKS = SEQ // P
TILES = BATCH * CHUNKS
FC = FF // P
SORTED = TILES + EXPERTS - 1
ROW = D + 2
NOBODY = 1 << 20
LN_EPS = 1e-5
RMS_EPS = 1e-6
TWO_PI_A = 6.28125
TWO_PI_B = float(2 * np.pi - TWO_PI_A)
ROUND = 1.5 * 2.0 ** 23
PI_IN = 3.1415925
WPIECE = 2048
PIECES = 2 * EXPERTS
KV, RT, Q, U = 0, 512, 520, 776
PCOLS = 4 * D + EXPERTS
XS = 256.0
SLOT = 1024
PEEL = 6
MOE_PEEL = 7
MOE_ROWS = 8
PADS = SORTED - TILES


def need(engine, sem, count):
    if not isinstance(count, int) or count > 0:
        engine.wait_ge(sem, count)


def live(t, n):
    return not isinstance(t, int) or 0 <= t < n


def steps(eng, n, lead, lag, step):
    pairs = (n - lead - PEEL) // 2
    for t in range(-lead, PEEL):
        step(t, t & 1)
    with eng.Fori(0, pairs) as k:
        step(k * 2 + PEEL, 0)
        step(k * 2 + PEEL + 1, 1)
    for t in range(PEEL + 2 * pairs, n + lag):
        step(t, t & 1)


def moe_steps(eng, lag, step):
    assert (SORTED - MOE_PEEL) % MOE_ROWS == 0
    for t in range(MOE_PEEL):
        step(t, t)
    with eng.Fori(0, (SORTED - MOE_PEEL) // MOE_ROWS) as k:
        for u in range(MOE_ROWS):
            step(k * MOE_ROWS + MOE_PEEL + u, (MOE_PEEL + u) % MOE_ROWS)
    for t in range(SORTED, SORTED + lag):
        step(t, t % MOE_ROWS)


def view(t, off, cols):
    return t[:, bass.ds(off, cols)]


def build(nc, x, slope, wqkvu, bqkvu, wout, bout, theta, wexp, b1, b2, out, xn_d, sorted_d):
    ctx = ExitStack()
    with ctx:
        def sb(name, cols, dt=F32):
            return ctx.enter_context(nc.sbuf_tensor(name, [P, cols], dt))

        region = sb("region", PIECES * WPIECE)
        at = [0]

        def part(cols):
            at[0] += cols
            return region[:, at[0] - cols:at[0]]

        ring = part(CHUNKS * SLOT)
        cos_all = part(CHUNKS * D)
        sin_all = part(CHUNKS * D)
        states = part((CHUNKS + 1) * D)
        masked = part(2 * HEADS * P)
        qT = part(2 * 512)
        kT_now = part(512)
        v_now = part(D)
        assert at[0] <= PIECES * WPIECE
        angle, size, turns = (masked[:, 0:1024], masked[:, 1024:2048], qT)

        xy = sb("xy", CHUNKS * D)
        work = sb("work", 5392)
        w_hi = work[:, 0:1032].bitcast(F16)
        w_lo = work[:, 1032:2064].bitcast(F16)
        wo_sb, mask, rot, w_now, w_term = (work[:, a:b] for a, b in (
            (2064, 2576), (2576, 3600), (3600, 4624), (4624, 5136), (5136, 5392)))
        theta_row = rot[:, 0:D]
        small = sb("small", 1792)
        xn, act_k, oT, osq, zT = (small[:, a:b] for a, b in (
            (0, 512), (512, 1024), (1024, 1280), (1280, 1536), (1536, 1792)))
        qbd = sb("qbd", 1024)
        rows_buf = sb("rows_buf", 4 * ROW)
        stg = sb("stg", 2 * WPIECE)
        moe_x = [work[:, k * D:(k + 1) * D].bitcast(F16) for k in range(2)]
        moe_h = work[:, 512:1536]
        moe_hh = [work[:, 1536 + k * 1024:2560 + k * 1024].bitcast(F16) for k in range(2)]
        moe_y = [work[:, 3584 + k * D:3840 + k * D] for k in range(4)]
        moe_s = work[:, 4608:4608 + D]
        moe_rows = [xy[:, k * ROW:(k + 1) * ROW] for k in range(MOE_ROWS)]
        b2_rows = stg[:, 0:EXPERTS * D]

        es_row = sb("es_row", D)
        bout_row = sb("bout_row", D)
        ident = sb("ident", P)
        ones = sb("ones", P)
        upper = sb("upper", P)
        ones_s = sb("ones_s", P, BF16)
        bias_p = sb("bias_p", 4 * D, BF16)
        neghalf = sb("neghalf", 1)
        halfpi = sb("halfpi", 1)
        pad_row = sb("pad_row", ROW)
        st6 = sb("st6", 12)
        mv = sb("mv", 4)
        vare = sb("vare", 2)
        rstd = sb("rstd", 2)
        mse = sb("mse", 2)
        rms = sb("rms", 2)
        slope_bc = sb("slope_bc", HEADS)
        es = sb("es", HEADS)
        pos0 = sb("pos0", CHUNKS)
        logits = sb("logits", TILES * EXPERTS)
        posi = sb("posi", TILES, U32)
        pad_posi = sb("pad_posi", PADS, U32)
        starts = sb("starts", SORTED)
        exp_of = sb("exp_of", SORTED, I32)
        tag = sb("tag", 2 * TILES)
        ini = sb("ini", SORTED, I32)
        ids = sb("ids", 4, U32)
        ssq = sb("ssq", PIECES + 1)
        tot = sb("tot", PIECES + 1)
        expo = sb("expo", PIECES + 1, I32)
        scale = sb("scale", PIECES + 1)
        inv = sb("inv", PIECES + 1)
        inv_p = sb("inv_p", 1)
        b1_cols = sb("b1_cols", EXPERTS * FC)
        b1_sq = sb("b1_sq", EXPERTS * FC)
        hsc = sb("hsc", 8 * EXPERTS)

        ps = [ctx.enter_context(nc.psum_tensor(f"bank{i}", [P, 512], F32)) for i in range(8)]

        S = {}
        for n in """const_in wp_in xn_ready xT_psum xhi_ready xlo_ready kv_psum k_act v_ready lg_ready rope_k kT_psum kT_ready
            k_now v_now state_psum state_ready stat var_ready rstd_ready pad_set pad_out q_psum q_act rope_q qT_psum
            q_moved s_psum s_masked w_part w_ready u_psum o_psum o_moved z_ready ms_psum ms_ready rms_ready xb_ready
            y_psum y_ready gp_const tab sines mask_part rows bias_t bias_in es_ready
            route_a pad_step route_act route_pe route_b disp_tag ssq_ready tot_ready scale_step scale_ready hi_ready lo_ready
            b_late b1_sum b1_tot xt_psum moe_xhi moe_xlo h_psum h_ready hhi_ready hlo_ready ye_psum y_summed ye_ready
            ids_ready""".split():
            S[n] = ctx.enter_context(nc.semaphore(n))
        for n, k in (("x_in", 2), ("xn_out", 2), ("row_out", 2), ("disp_in", 4), ("disp_out", 4), ("w_in", 2),
                     ("xs_in", MOE_ROWS), ("ye_out", 4)):
            S[n] = [ctx.enter_context(nc.semaphore(f"{n}{i}")) for i in range(k)]

        block = ctx.enter_context(nc.Block())

        def piece_parts(k):
            p = region[:, k * WPIECE:(k + 1) * WPIECE].bitcast(F16)
            return p[:, 0:WPIECE], p[:, WPIECE:2 * WPIECE]

        @block.sync
        def _(sp):
            sp.dma_start(stg[:, 0:2 * PCOLS], wqkvu).then_inc(S["wp_in"], 16)

            for b in range(BATCH):
                def step_a(t, par, b=b):
                    i = t + 4
                    if live(i, CHUNKS):
                        g = b * CHUNKS + i
                        need(sp, S["x_in"][par], 8 * (g - par))
                        if b:
                            sp.wait_ge(S["row_out"][par], 8 * (i - par) + 16)
                        sp.dma_start(view(xy, i * D, D), x[bass.ds(g * P, P), :]).then_inc(S["x_in"][par], 16)
                    if live(t, CHUNKS):
                        g = b * CHUNKS + t
                        sp.wait_ge(S["xn_ready"], g + 1)
                        sp.dma_start(xn_d[bass.ds(g * P, P), :], xn[:, par * D:(par + 1) * D]).then_inc(S["xn_out"][par], 16)
                steps(sp, CHUNKS, 4, 0, step_a)

                def step_b(t, par, b=b):
                    if live(t, CHUNKS):
                        g = b * CHUNKS + t
                        need(sp, S["s_psum"], 2 * g)
                        sp.wait_ge(S["kT_ready"], (b + 1) * CHUNKS)
                        sp.dma_start(kT_now, view(ring, t * SLOT, 512)).then_inc(S["k_now"], 16)
                    i = t - 4
                    if live(i, CHUNKS):
                        g = b * CHUNKS + i
                        sp.wait_ge(S["y_ready"], g + 1)
                        need(sp, S["row_out"][par], 8 * (g - par))
                        sp.dma_start(out[bass.ds(g * P, P), :], view(xy, i * D, D)).then_inc(S["row_out"][par], 16)
                    i = t - 1
                    if live(i, CHUNKS):
                        g = b * CHUNKS + i
                        need(sp, S["o_psum"], g)
                        sp.dma_start(v_now, view(ring, i * SLOT + 512, D)).then_inc(S["v_now"], 16)
                sp.wait_ge(S["v_ready"], (b + 1) * CHUNKS)
                steps(sp, CHUNKS, 0, 4, step_b)

            for k in range(PIECES):
                sp.wait_ge(S["lo_ready"], max(k, 1))
                sp.wait_ge(S["hi_ready"], max(k, 1))
                sp.dma_start(stg[:, (k % 2) * WPIECE:(k % 2 + 1) * WPIECE], wexp[:, k * WPIECE:(k + 1) * WPIECE]).then_inc(S["w_in"][k % 2], 16)

            for slot in range(4):
                sp.wait_ge(S["disp_out"][slot], 16 * TILES // 4)
            sp.wait_ge(S["pad_out"], 16 * PADS)
            for q in range(2):
                sp.wait_ge(S["row_out"][q], 8 * TILES)

            def load_sorted(t, slot):
                need(sp, S["ye_ready"], t - 6)
                need(sp, S["ids_ready"], t - 6)
                sp.dma_start(moe_rows[slot], sorted_d[bass.ds(t * P, P), :]).then_inc(S["xs_in"][slot], 16)
            moe_steps(sp, 0, load_sorted)

        @block.gpsimd
        def _(gp):
            K = S["gp_const"]
            gp.iota(ini[:, 0:CHUNKS], [[P, CHUNKS]], base=0, channel_multiplier=1).then_inc(K, 1)
            gp.wait_ge(K, 1)
            gp.tensor_copy(pos0[:, :], ini[:, 0:CHUNKS]).then_inc(K, 1)
            gp.memset(halfpi[:, :], float(np.pi / 2)).then_inc(K, 1)
            gp.memset(ident[:, :], 0.0).then_inc(K, 1)
            gp.memset(ones[:, :], 1.0).then_inc(K, 1)
            gp.memset(neghalf[:, :], -0.5).then_inc(K, 1)
            gp.wait_ge(K, 6)
            gp.affine_select(out=ident[:, :], in_=ident[:, :], compare_op=ALU.not_equal, fill=1.0,
                             base=0, pattern=[[-1, P]], channel_multiplier=1).then_inc(K, 1)
            gp.affine_select(out=upper[:, :], in_=ones[:, :], compare_op=ALU.is_gt, fill=0.0,
                             base=0, pattern=[[1, P]], channel_multiplier=-1).then_inc(K, 1)
            gp.wait_ge(K, 8)
            gp.wait_ge(S["ssq_ready"], 1)
            gp.partition_all_reduce(tot[:, PIECES:PIECES + 1], ssq[:, PIECES:PIECES + 1], P, bass.bass_isa.ReduceOp.add).then_inc(S["tot_ready"], 1)
            B = S["bias_t"]
            temp, low = small[:, 0:1024], small[:, 1024:1536].bitcast(BF16)
            gp.memset(temp, 0.0).then_inc(B, 1)
            gp.wait_ge(B, 1)
            for q in range(3):
                gp.dma_start(temp[32 * q:32 * q + 1, :], bqkvu[0:1, :]).then_inc(S["bias_in"], 16)
            gp.wait_ge(S["bias_in"], 48)
            gp.tensor_copy(bias_p[:, :], temp).then_inc(B, 1)
            gp.wait_ge(B, 2)
            gp.tensor_tensor(temp, temp, bias_p[:, :], ALU.subtract).then_inc(B, 1)
            gp.wait_ge(B, 3)
            gp.tensor_copy(low, temp).then_inc(B, 1)
            gp.wait_ge(B, 4)
            gp.tensor_tensor(temp, temp, low, ALU.subtract).then_inc(B, 1)
            gp.wait_ge(B, 5)
            gp.tensor_copy(bias_p[32:33, :], low[32:33, :]).then_inc(B, 1)
            gp.wait_ge(B, 6)
            gp.tensor_copy(bias_p[64:65, :], temp[64:65, :]).then_inc(B, 1)

            def deviation(b, t, par):
                g = b * CHUNKS + t
                need(gp, S["xn_ready"], g - 1)
                gp.wait_ge(S["var_ready"], g + 1)
                gp.tensor_tensor(rstd[:, par:par + 1], vare[:, par:par + 1], neghalf[:, :], ALU.pow).then_inc(S["rstd_ready"], 1)

            gp.wait_ge(B, 7)
            deviation(0, 0, 0)
            deviation(0, 1, 1)
            gp.memset(states[:, :], 0.0).then_inc(K, 1)
            gp.memset(qbd[:, :], 0.0).then_inc(K, 1)
            gp.iota(tag[:, :].bitcast(I32).rearrange("p (t c) -> p t c", c=2)[:, :, 1:2], [[P, TILES], [0, 1]], base=0,
                    channel_multiplier=1).then_inc(K, 1)
            gp.iota(ini[:, :], [[P, SORTED]], base=0, channel_multiplier=0).then_inc(K, 1)
            gp.wait_ge(K, 12)
            gp.tensor_copy(starts[:, :], ini[:, :]).then_inc(K, 1)
            gp.memset(pad_row[:, :], 0.0).then_inc(S["pad_set"], 1)
            gp.wait_ge(S["pad_set"], 1)
            gp.memset(pad_row[:, D + 1:D + 2].bitcast(I32), NOBODY).then_inc(S["pad_set"], 1)

            for b in range(BATCH):
                for t in range(2 if b == 0 else 0, 4):
                    deviation(b, t, t & 1)
                with gp.Fori(0, (CHUNKS - 4) // 2) as k:
                    deviation(b, k * 2 + 4, 0)
                    deviation(b, k * 2 + 5, 1)

                def step_b(t, par, b=b):
                    i = t - 1
                    if live(i, CHUNKS):
                        g = b * CHUNKS + i
                        w = w_now[:, (1 - par) * D:(2 - par) * D]
                        need(gp, S["o_psum"], g - 1)
                        need(gp, S["w_ready"], g)
                        gp.tensor_tensor(w, states[:, CHUNKS * D:(CHUNKS + 1) * D], view(states, (i + 1) * D, D),
                                         ALU.subtract).then_inc(S["w_part"], 1)
                        gp.tensor_tensor(w_term, view(states, i * D, D), es_row[:, :], ALU.mult).then_inc(S["w_part"], 1)
                        gp.wait_ge(S["w_part"], 2 * g + 2)
                        gp.tensor_tensor(w, w, w_term, ALU.add).then_inc(S["w_ready"], 1)
                    if live(t, CHUNKS):
                        gp.tensor_tensor(view(xy, t * D, D), view(xy, t * D, D), bout_row[:, :], ALU.add).then_inc(S["xb_ready"], 1)
                    i = t - 3
                    if live(i, CHUNKS):
                        g = b * CHUNKS + i
                        q = 1 - par
                        need(gp, S["y_ready"], g - 1)
                        gp.wait_ge(S["ms_ready"], g + 1)
                        gp.tensor_tensor(rms[:, q:q + 1], mse[:, q:q + 1], neghalf[:, :], ALU.pow).then_inc(S["rms_ready"], 1)
                    if b == BATCH - 1 and isinstance(t, int) and 0 <= t < CHUNKS:
                        for r in (2 * t, 2 * t + 1):
                            dst = rows_buf[:, (r % 4) * ROW:(r % 4 + 1) * ROW]
                            gp.wait_ge(S["disp_in"][r % 4], 16 * (r // 4 + 1))
                            gp.tensor_copy(dst[:, D:D + 2].bitcast(U32), tag[:, 2 * r:2 * r + 2].bitcast(U32)).then_inc(S["disp_tag"], 1)
                            gp.wait_ge(S["disp_tag"], r + 1)
                            gp.indirect_dma_start(sorted_d[:, :], bass.IndirectOffsetOnAxis(ap=posi[:, r:r + 1], axis=0),
                                                  dst, None).then_inc(S["disp_out"][r % 4], 16)
                        if t < PADS:
                            gp.wait_ge(S["pad_set"], 2)
                            gp.indirect_dma_start(sorted_d[:, :], bass.IndirectOffsetOnAxis(ap=pad_posi[:, t:t + 1], axis=0),
                                                  pad_row[:, :], None).then_inc(S["pad_out"], 16)
                gp.wait_ge(S["state_ready"], 2 * (b + 1) * CHUNKS)
                gp.wait_ge(S["rows"], 2)
                gp.wait_ge(S["const_in"], 80)
                if b < BATCH - 1:
                    steps(gp, CHUNKS, 0, 3, step_b)
                else:
                    gp.wait_ge(S["route_b"], 3)
                    for t in range(CHUNKS + 3):
                        step_b(t, t & 1)

            for k in range(PIECES):
                gp.wait_ge(S["ssq_ready"], k + 2)
                gp.partition_all_reduce(tot[:, k:k + 1], ssq[:, k:k + 1], P, bass.bass_isa.ReduceOp.add).then_inc(S["tot_ready"], 1)
            gp.wait_ge(S["b1_sum"], 2)
            gp.partition_all_reduce(hsc[:, 8:16], hsc[:, 0:8], P, bass.bass_isa.ReduceOp.add).then_inc(S["b1_tot"], 1)

            for q in range(2):
                gp.wait_ge(S["row_out"][q], 8 * TILES)
            last_row = gp.to_reg(TILES * P - 1)
            for t in range(SORTED):
                slot = t % 4
                gp.wait_ge(S["ye_ready"], t + 1)
                gp.wait_ge(S["ids_ready"], t + 1)
                gp.indirect_dma_start(out[:, :], bass.IndirectOffsetOnAxis(ap=ids[:, slot:slot + 1], axis=0),
                                      moe_y[slot], None, bounds_check=last_row, oob_is_err=False,
                                      compute_op=ALU.add).then_inc(S["ye_out"][slot], 16)
            for slot in range(4):
                gp.wait_ge(S["ye_out"][slot], 16 * len(range(slot, SORTED, 4)))

        @block.scalar
        def _(act):
            C = S["const_in"]
            act.dma_start(theta_row, theta[0:1, :].broadcast_to([P, D])).then_inc(C, 16)
            act.dma_start(slope_bc[:, :], slope[0:1, :].broadcast_to([P, HEADS])).then_inc(C, 16)
            act.dma_start(wo_sb, wout).then_inc(C, 16)
            act.dma_start(bout_row[:, :], bout[0:1, :].broadcast_to([P, D])).then_inc(C, 16)
            act.dma_start(b1_cols[:, :], b1).then_inc(C, 16)
            act.wait_ge(C, 80)
            act.activation(es[:, :], slope_bc[:, :], ACT.Exp).then_inc(S["es_ready"], 1)
            act.wait_ge(S["wp_in"], 16)
            act.activation(w_hi, stg[:, 0:2 * PCOLS], ACT.Square, accum_out=ssq[:, PIECES:PIECES + 1]).then_inc(S["ssq_ready"], 1)

            def sines(q):
                r = angle
                act.wait_ge(S["tab"], 6 * q + 6)
                act.wait_ge(S["gp_const"], 3)
                act.activation(sin_all[:, q * 1024:(q + 1) * 1024], r, ACT.Sin).then_inc(S["sines"], 1)
                need(act, S["sines"], 3 * q)
                act.activation(size, r, ACT.Abs).then_inc(S["sines"], 1)
                act.wait_ge(S["sines"], 3 * q + 2)
                act.activation(cos_all[:, q * 1024:(q + 1) * 1024], size, ACT.Sin, scale=-1.0,
                               bias=halfpi[:, 0:1]).then_inc(S["sines"], 1)

            sines(0)
            act.wait_ge(S["scale_ready"], 1)
            act.activation(w_hi, stg[:, 0:2 * PCOLS], ACT.Copy, scale=scale[:, PIECES:PIECES + 1]).then_inc(S["hi_ready"], 1)
            for q in range(1, 4):
                sines(q)

            for b in range(BATCH):
                def step_a(t, par, b=b):
                    if live(t, CHUNKS):
                        g = b * CHUNKS + t
                        act.wait_ge(S["xT_psum"], g + 1)
                        act.activation(view(ring, t * SLOT + 768, P).bitcast(F16), ps[0][:, 0:D], ACT.Copy,
                                       scale=XS).then_inc(S["xhi_ready"], 1)
                    i = t - 1
                    if live(i, CHUNKS):
                        g = b * CHUNKS + i
                        q = 1 - par
                        act.wait_ge(S["kv_psum"], g + 1)
                        need(act, S["rope_k"], 2 * (g - 1))
                        act.activation(act_k[:, q * D:(q + 1) * D], ps[1][:, 0:D], ACT.Silu, scale=inv_p[:, :]).then_inc(S["k_act"], 1)
                        act.activation(view(ring, i * SLOT + 512, D), ps[1][:, D:2 * D], ACT.Copy, scale=inv_p[:, :]).then_inc(S["v_ready"], 1)
                        act.activation(view(logits, g * EXPERTS, EXPERTS), ps[2][:, 0:EXPERTS],
                                       ACT.Copy, scale=inv_p[:, :]).then_inc(S["lg_ready"], 1)
                    i = t - 2
                    if live(i, CHUNKS):
                        g = b * CHUNKS + i
                        act.wait_ge(S["kT_psum"], g + 1)
                        act.activation(view(ring, i * SLOT, 512), ps[3][:, :], ACT.Copy).then_inc(S["kT_ready"], 1)
                if b:
                    act.wait_ge(S["s_psum"], 2 * b * CHUNKS)
                    act.wait_ge(S["o_psum"], b * CHUNKS)
                    act.wait_ge(S["rope_q"], 2 * b * CHUNKS)
                else:
                    act.wait_ge(S["scale_ready"], 2)
                steps(act, CHUNKS, 0, 2, step_a)

                if b == BATCH - 1:
                    act.wait_ge(S["route_a"], 8)
                    act.activation(small[:, 320:576], small[:, 64:320], ACT.Exp).then_inc(S["route_act"], 1)
                    for q in range(2):
                        act.wait_ge(S["xn_out"][q], 8 * TILES)

                def step_b(t, par, b=b):
                    i = t - 1
                    if live(i, CHUNKS):
                        g = b * CHUNKS + i
                        q = 1 - par
                        act.wait_ge(S["qT_psum"], g + 1)
                        need(act, S["s_psum"], 2 * g)
                        for h in range(2):
                            act.activation(qbd[64 * h:64 * h + 64, :].rearrange("p (a h n) -> p a h n", a=4, h=2)[:, :, h, :],
                                           ps[0][64 * h:64 * h + 64, :].rearrange("p (a n) -> p a n", a=4),
                                           ACT.Copy).then_inc(S["q_moved"], 1)
                        need(act, S["o_psum"], g - 1)
                        act.activation(qT[:, q * 512:(q + 1) * 512], ps[0][:, :], ACT.Copy).then_inc(S["q_moved"], 1)
                    if live(t, CHUNKS):
                        g = b * CHUNKS + t
                        act.wait_ge(S["q_psum"], g + 1)
                        need(act, S["rope_q"], 2 * (g - 1))
                        act.activation(act_k[:, par * D:(par + 1) * D], ps[1 + par][:, 0:D], ACT.Silu, scale=inv_p[:, :]).then_inc(S["q_act"], 1)
                    i = t - 2
                    if live(i, CHUNKS):
                        g = b * CHUNKS + i
                        act.wait_ge(S["o_psum"], g + 1)
                        need(act, S["z_ready"], 2 * g)
                        act.activation(oT, ps[5][:, 0:D], ACT.Copy).then_inc(S["o_moved"], 1)
                        need(act, S["ms_psum"], g)
                        act.activation(osq, ps[5][:, 0:D], ACT.Square).then_inc(S["o_moved"], 1)
                    if b == BATCH - 1 and isinstance(t, int) and 0 <= t < CHUNKS:
                        for r in (2 * t, 2 * t + 1):
                            need(act, S["disp_out"][r % 4], 16 * (r // 4))
                            act.dma_start(rows_buf[:, (r % 4) * ROW:(r % 4) * ROW + D], xn_d[r * P:(r + 1) * P, :]).then_inc(S["disp_in"][r % 4], 16)
                act.wait_ge(S["rope_k"], 2 * (b + 1) * CHUNKS)
                act.wait_ge(S["gp_const"], 10)
                if b < BATCH - 1:
                    steps(act, CHUNKS, 0, 2, step_b)
                else:
                    act.wait_ge(S["route_b"], 3)
                    for t in range(CHUNKS + 2):
                        step_b(t, t & 1)

            act.wait_ge(S["o_psum"], TILES)
            for k in range(PIECES):
                hi, lo = piece_parts(k)
                src = stg[:, (k % 2) * WPIECE:(k % 2 + 1) * WPIECE]
                act.wait_ge(S["w_in"][k % 2], 16 * (k // 2 + 1))
                act.activation(hi, src, ACT.Square, accum_out=ssq[:, k:k + 1]).then_inc(S["ssq_ready"], 1)
                act.wait_ge(S["scale_ready"], k + 3)
                act.activation(hi, src, ACT.Copy, scale=scale[:, k:k + 1]).then_inc(S["hi_ready"], 1)
            act.wait_ge(S["lo_ready"], PIECES)
            act.dma_start(b2_rows, b2[0:1, :].broadcast_to([P, EXPERTS * D])).then_inc(S["b_late"], 16)

            def step(t, m):
                if live(t, SORTED):
                    act.wait_ge(S["xt_psum"], t + 1)
                    need(act, S["h_psum"], 2 * (t - 1))
                    act.activation(moe_x[m % 2][:, 0:D], ps[0][:, 0:D], ACT.Copy, scale=XS).then_inc(S["moe_xhi"], 1)
                i = t - 1
                if live(i, SORTED):
                    for n in range(2):
                        act.wait_ge(S["h_ready"], 2 * i + n + 1)
                        need(act, S["ye_psum"], i - 1)
                        act.activation(moe_hh[(m - 1) % 2][:, n * 512:(n + 1) * 512], moe_h[:, n * 512:(n + 1) * 512],
                                       ACT.Relu).then_inc(S["hhi_ready"], 1)
                i = t - 3
                if live(i, SORTED):
                    k, r = (m - 3) % 4, (m - 3) % MOE_ROWS
                    act.wait_ge(S["y_summed"], i + 1)
                    need(act, S["ye_out"][k], 4 * (i - k))
                    act.activation(moe_y[k], moe_s, ACT.Copy, scale=moe_rows[r][:, D:D + 1]).then_inc(S["ye_ready"], 1)
            moe_steps(act, 3, step)

        @block.vector
        def _(dve):
            v = nc.vector
            T = S["tab"]

            def table(q):
                need(dve, S["sines"], 3 * q)
                for k in range(4):
                    c = 4 * q + k
                    ins = v.tensor_scalar(angle[:, k * D:(k + 1) * D], theta_row, pos0[:, c:c + 1], None, ALU.mult)
                ins.then_inc(T, 1)
                dve.wait_ge(T, 6 * q + 1)
                v.tensor_scalar(turns, angle, float(1 / (2 * np.pi)), ROUND, ALU.mult, ALU.add).then_inc(T, 1)
                dve.wait_ge(T, 6 * q + 2)
                v.tensor_scalar(turns, turns, ROUND, None, ALU.subtract).then_inc(T, 1)
                for n, turn in enumerate((TWO_PI_A, TWO_PI_B)):
                    dve.wait_ge(T, 6 * q + 3 + n)
                    v.scalar_tensor_tensor(angle, turns, -turn, angle, ALU.mult, ALU.add).then_inc(T, 1)
                dve.wait_ge(T, 6 * q + 5)
                v.tensor_scalar(angle, angle, PI_IN, -PI_IN, ALU.min, ALU.max).then_inc(T, 1)

            E = S["scale_step"]
            count = [0]

            def chain(ins):
                count[0] += 1
                ins.then_inc(E, 1)
                dve.wait_ge(E, count[0])

            def power(total, e, up, down, done=None):
                chain(v.tensor_scalar(e, total.bitcast(I32), 23, None, ALU.logical_shift_right))
                chain(v.tensor_scalar(e, e, 3.0, None, ALU.add))
                chain(v.tensor_scalar(e, e, 1, None, ALU.logical_shift_right))
                chain(v.tensor_scalar(up.bitcast(I32), e, -1.0, 206.0, ALU.mult, ALU.add))
                chain(v.tensor_scalar(up.bitcast(I32), up.bitcast(I32), 23, None, ALU.logical_shift_left))
                chain(v.tensor_scalar(e, e, 48.0, None, ALU.add))
                last = v.tensor_scalar(down.bitcast(I32), e, 23, None, ALU.logical_shift_left)
                if done is None:
                    chain(last)
                else:
                    last.then_inc(done, 1)

            def routing(dve):
                A, F = S["route_a"], S["pad_step"]

                def cols(a, n):
                    return small[:, a:a + n]

                def by_tile(ap):
                    return ap.rearrange("p (t e) -> p t e", e=EXPERTS)

                def per_tile(ap):
                    return ap.rearrange("p (t a) -> p t a", a=1).broadcast_to([P, TILES, EXPERTS])

                TE = TILES * EXPERTS
                top, less, ex = cols(32, TILES), cols(64, TE), cols(320, TE)
                pick, rank, red, onehot = cols(576, TE), cols(832, EXPERTS), cols(840, TILES), cols(872, TE)
                one, padded, ends, over = cols(1128, TILES), cols(1168, EXPERTS), cols(1176, EXPERTS), cols(1184, SORTED * EXPERTS)
                passed = cols(1500, SORTED)
                count_f, till, before, pad_sum = (cols(1544 + 8 * n, EXPERTS) for n in range(4))
                pad_over = cols(1576, PADS * EXPERTS)
                incl = pick
                L = by_tile(logits[:, :])
                dve.wait_ge(S["lg_ready"], TILES)
                for q in range(2):
                    dve.wait_ge(S["xn_out"][q], 8 * TILES)
                v.reduce_max(top, L, AX.X).then_inc(A, 1)
                for e in range(EXPERTS):
                    ins = v.memset(rank[:, e:e + 1], float(EXPERTS - e))
                ins.then_inc(A, 1)
                dve.wait_ge(A, 2)
                v.tensor_tensor(by_tile(less), L, per_tile(top), ALU.subtract).then_inc(A, 1)
                v.tensor_tensor(by_tile(pick), L, per_tile(top), ALU.is_equal).then_inc(A, 1)
                dve.wait_ge(A, 4)
                v.tensor_tensor(by_tile(pick), by_tile(pick),
                                rank.rearrange("p (a e) -> p a e", a=1).broadcast_to([P, TILES, EXPERTS]), ALU.mult).then_inc(A, 1)
                dve.wait_ge(A, 5)
                v.reduce_max(red, by_tile(pick), AX.X).then_inc(A, 1)
                dve.wait_ge(A, 6)
                v.tensor_tensor(onehot.rearrange("p (e t) -> p t e", e=EXPERTS), by_tile(pick), per_tile(red),
                                ALU.is_equal).then_inc(A, 1)
                v.memset(one, 1.0).then_inc(A, 1)
                dve.wait_ge(A, 8)
                dve.wait_ge(S["route_pe"], 2)
                for e in range(EXPERTS):
                    ins = v.tensor_tensor_scan(incl[:, e * TILES:(e + 1) * TILES], one,
                                               ps[4][:, e * TILES:(e + 1) * TILES], 0.0, ALU.mult, ALU.add)
                ins.then_inc(A, 1)
                dve.wait_ge(A, 9)
                i3 = incl.rearrange("p (e t) -> p e t", e=EXPERTS)
                whole = exp_of[:, 0:EXPERTS]
                v.tensor_scalar(whole, i3[:, :, TILES - 1], float(P - 1), None, ALU.add).then_inc(A, 1)
                v.tensor_copy(count_f, i3[:, :, TILES - 1]).then_inc(F, 1)
                dve.wait_ge(A, 10)
                dve.wait_ge(F, 1)
                v.tensor_tensor(incl, incl, ps[4][:, 0:TE], ALU.subtract).then_inc(A, 1)
                dve.wait_ge(A, 11)
                shift = P.bit_length() - 1
                v.tensor_scalar(whole, whole, shift, shift, ALU.logical_shift_right, ALU.logical_shift_left).then_inc(A, 1)
                v.tensor_tensor(incl, incl, ps[3][:, 0:TE], ALU.add).then_inc(A, 1)
                dve.wait_ge(A, 13)
                v.tensor_copy(padded, whole).then_inc(A, 1)
                dve.wait_ge(A, 14)
                v.tensor_tensor_scan(ends, one[:, 0:EXPERTS], padded, 0.0, ALU.mult, ALU.add).then_inc(A, 1)
                dve.wait_ge(A, 15)
                v.tensor_tensor(padded, ends, padded, ALU.subtract).then_inc(A, 1)
                dve.wait_ge(A, 16)
                v.tensor_tensor(i3, i3, padded.rearrange("p (e a) -> p e a", a=1).broadcast_to([P, EXPERTS, TILES]),
                                ALU.add).then_inc(A, 1)
                dve.wait_ge(A, 17)
                v.tensor_tensor(incl, incl, onehot, ALU.mult).then_inc(A, 1)
                dve.wait_ge(A, 18)
                v.reduce_sum(red, incl.rearrange("p (e t) -> p t e", e=EXPERTS), AX.X).then_inc(A, 1)
                dve.wait_ge(S["gp_const"], 13)
                v.tensor_tensor(over.rearrange("p (j e) -> p j e", e=EXPERTS),
                                ends.rearrange("p (a e) -> p a e", a=1).broadcast_to([P, SORTED, EXPERTS]),
                                starts[:, :].rearrange("p (j a) -> p j a", a=1).broadcast_to([P, SORTED, EXPERTS]),
                                ALU.is_le).then_inc(A, 1)
                dve.wait_ge(A, 20)
                v.tensor_copy(posi[:, :], red).then_inc(A, 1)
                v.reduce_sum(passed, over.rearrange("p (j e) -> p j e", e=EXPERTS), AX.X).then_inc(A, 1)
                dve.wait_ge(A, 22)
                v.tensor_scalar(exp_of[:, :], passed, float(EXPERTS - 1), None, ALU.min).then_inc(S["route_b"], 1)
                v.tensor_tensor_scan(till, one[:, 0:EXPERTS], count_f, 0.0, ALU.mult, ALU.add).then_inc(F, 1)
                dve.wait_ge(F, 2)
                v.tensor_tensor(before, padded, till, ALU.subtract).then_inc(F, 1)
                dve.wait_ge(F, 3)
                v.tensor_tensor(before, before, count_f, ALU.add).then_inc(F, 1)
                dve.wait_ge(F, 4)
                po = pad_over.rearrange("p (j e) -> p j e", e=EXPERTS)
                v.tensor_tensor(po, before.rearrange("p (a e) -> p a e", a=1).broadcast_to([P, PADS, EXPERTS]),
                                pos0[:, 0:PADS].rearrange("p (j a) -> p j a", a=1).broadcast_to([P, PADS, EXPERTS]),
                                ALU.is_le).then_inc(F, 1)
                dve.wait_ge(F, 5)
                v.tensor_tensor(po, po, count_f.rearrange("p (a e) -> p a e", a=1).broadcast_to([P, PADS, EXPERTS]),
                                ALU.mult).then_inc(F, 1)
                dve.wait_ge(F, 6)
                v.reduce_sum(pad_sum[:, 0:PADS], po, AX.X).then_inc(F, 1)
                dve.wait_ge(F, 7)
                v.tensor_tensor(pad_sum[:, 0:PADS], pad_sum[:, 0:PADS], pos0[:, 0:PADS], ALU.add).then_inc(F, 1)
                dve.wait_ge(F, 8)
                v.tensor_copy(pad_posi[:, :], pad_sum[:, 0:PADS]).then_inc(S["route_b"], 1)
                dve.wait_ge(S["route_act"], 1)
                v.reduce_sum(red, by_tile(ex), AX.X).then_inc(A, 1)
                dve.wait_ge(A, 23)
                v.reciprocal(tag[:, 0::2], red).then_inc(S["route_b"], 1)

            def statistics(b, t, par):
                g = b * CHUNKS + t
                dve.wait_ge(S["x_in"][par], 8 * (g - par) + 16)
                v.bn_stats(st6[:, 6 * par:6 * par + 6], view(xy, t * D, D)).then_inc(S["stat"], 1)
                dve.wait_ge(S["stat"], 2 * g + 1)

            def variance(b, t, par):
                g = b * CHUNKS + t
                v.bn_aggr(mv[:, 2 * par:2 * par + 2], st6[:, 6 * par:6 * par + 6]).then_inc(S["stat"], 1)
                dve.wait_ge(S["stat"], 2 * g + 2)
                need(dve, S["rstd_ready"], g - 1)
                v.tensor_scalar(vare[:, par:par + 1], mv[:, 2 * par + 1:2 * par + 2], LN_EPS, None, ALU.add).then_inc(S["var_ready"], 1)

            def rope(src, dst, c, done):
                d4 = dst.rearrange("p (h s d) -> p h s d", h=HEADS, s=2)
                s3 = src.rearrange("p (h d) -> p h d", d=HD)
                for n, tab in enumerate((cos_all, sin_all)):
                    v.tensor_tensor(d4[:, :, n, :], s3, view(tab, c * D, D).rearrange("p (h d) -> p h d", d=HD),
                                    ALU.mult).then_inc(done, 1)

            dve.wait_ge(S["const_in"], 80)
            dve.wait_ge(S["gp_const"], 2)
            table(0)
            dve.wait_ge(S["tot_ready"], 1)
            pr = slice(PIECES, PIECES + 1)
            power(tot[:, pr], expo[:, pr], scale[:, pr], inv[:, pr])
            v.tensor_scalar(inv_p[:, :], inv[:, pr], 1.0 / XS, None, ALU.mult).then_inc(S["scale_ready"], 1)
            dve.wait_ge(S["gp_const"], 5)
            v.tensor_scalar(ones_s[:, :], ones[:, :], scale[:, pr], XS, ALU.mult, ALU.mult).then_inc(S["scale_ready"], 1)
            for t in range(2):
                statistics(0, t, t)
                variance(0, t, t)
            table(1)
            dve.wait_ge(S["hi_ready"], 1)
            v.scalar_tensor_tensor(w_lo, stg[:, 0:2 * PCOLS], scale[:, pr], w_hi, ALU.mult, ALU.subtract).then_inc(S["lo_ready"], 1)
            table(2)
            table(3)
            M = S["mask_part"]
            dve.wait_ge(S["es_ready"], 1)
            dve.wait_ge(S["gp_const"], 8)
            dve.wait_ge(S["bias_t"], 7)
            v.tensor_tensor(zT[:, 0:P], upper[:, :], ident[:, :], ALU.add).then_inc(M, 1)
            v.tensor_scalar(slope_bc[:, :], es[:, :], -1.0, None, ALU.add).then_inc(M, 1)
            dve.wait_ge(M, 2)
            for h in range(HEADS):
                ins = v.tensor_scalar(mask[:, h * P:(h + 1) * P], zT[:, 0:P], slope_bc[:, h:h + 1], 1.0, ALU.mult, ALU.add)
            ins.then_inc(S["rows"], 1)
            v.tensor_copy(es_row[:, :].rearrange("p (h d) -> p h d", d=HD),
                          es[:, :].rearrange("p (h a) -> p h a", a=1).broadcast_to([P, HEADS, HD])).then_inc(S["rows"], 1)
            dve.wait_ge(S["rows"], 2)
            dve.wait_ge(S["sines"], 12)
            dve.wait_ge(S["gp_const"], 9)

            for b in range(BATCH):
                def step_a(t, par, b=b):
                    i = t + 2
                    measured = live(i, CHUNKS) and not (b == 0 and isinstance(t, int) and i < 2)
                    if measured:
                        statistics(b, i, par)
                    i = t + 1
                    if live(i, CHUNKS):
                        g = b * CHUNKS + i
                        q = 1 - par
                        dve.wait_ge(S["rstd_ready"], g + 1)
                        need(dve, S["xT_psum"], g - 1)
                        need(dve, S["xn_out"][q], 8 * (g - q))
                        v.tensor_scalar(xn[:, q * D:(q + 1) * D], view(xy, i * D, D), mv[:, 2 * q:2 * q + 1], rstd[:, q:q + 1],
                                        ALU.subtract, ALU.mult).then_inc(S["xn_ready"], 1)
                    if measured:
                        variance(b, t + 2, par)
                    if live(t, CHUNKS):
                        g = b * CHUNKS + t
                        xh = view(ring, t * SLOT + 768, D).bitcast(F16)
                        dve.wait_ge(S["xhi_ready"], g + 1)
                        v.scalar_tensor_tensor(xh[:, D:2 * D], ps[0][:, 0:D], XS, xh[:, 0:D],
                                               ALU.mult, ALU.subtract).then_inc(S["xlo_ready"], 1)
                    i = t - 1
                    if live(i, CHUNKS):
                        g = b * CHUNKS + i
                        q = 1 - par
                        dve.wait_ge(S["k_act"], g + 1)
                        need(dve, S["state_psum"], g - 1)
                        rope(act_k[:, q * D:(q + 1) * D], rot[:, q * 512:(q + 1) * 512], i, S["rope_k"])
                    i = t - 2
                    if live(i, CHUNKS):
                        g = b * CHUNKS + i
                        dve.wait_ge(S["state_psum"], g + 1)
                        need(dve, S["state_ready"], 2 * g)
                        for h in range(2):
                            lo, hi = 64 * h, 64 * h + 64
                            one = ps[4][lo:hi, :].rearrange("p (g a c) -> p g a c", g=2, a=4)[:, :, 0:4:3, 32 * h:32 * h + 32]
                            before = states[lo:hi, bass.ds(i * D, D)].rearrange("p (g a c) -> p g a c", g=2, a=2)[:, :, :, 32 * h:32 * h + 32]
                            after = states[lo:hi, bass.ds((i + 1) * D, D)].rearrange("p (g a c) -> p g a c", g=2, a=2)[:, :, :, 32 * h:32 * h + 32]
                            v.tensor_tensor(after, one, before, ALU.add).then_inc(S["state_ready"], 1)
                if b:
                    dve.wait_ge(S["w_ready"], b * CHUNKS)
                    dve.wait_ge(S["qT_psum"], b * CHUNKS)
                    dve.wait_ge(S["o_psum"], b * CHUNKS)
                steps(dve, CHUNKS, 2, 2, step_a)
                if b == BATCH - 1:
                    routing(dve)

                def step_b(t, par, b=b):
                    if live(t, CHUNKS):
                        g = b * CHUNKS + t
                        dve.wait_ge(S["q_act"], g + 1)
                        need(dve, S["qT_psum"], g - 1)
                        rope(act_k[:, par * D:(par + 1) * D], rot[:, par * 512:(par + 1) * 512], t, S["rope_q"])
                    i = t - 1
                    if live(i, CHUNKS):
                        g = b * CHUNKS + i
                        q = 1 - par
                        need(dve, S["o_psum"], g - 1)
                        for n in range(2):
                            dve.wait_ge(S["s_psum"], 2 * g + n + 1)
                            v.tensor_tensor(masked[:, q * 1024 + n * 512:q * 1024 + (n + 1) * 512], ps[3 + n][:, :],
                                            mask[:, n * 512:(n + 1) * 512], ALU.mult).then_inc(S["s_masked"], 1)
                    i = t - 3
                    if live(i, CHUNKS):
                        g = b * CHUNKS + i
                        q = 1 - par
                        dve.wait_ge(S["ms_psum"], g + 1)
                        need(dve, S["rms_ready"], g - 1)
                        v.tensor_scalar(mse[:, q:q + 1], ps[6][:, D:D + 1], 1.0 / D, RMS_EPS, ALU.mult, ALU.add).then_inc(S["ms_ready"], 1)
                        dve.wait_ge(S["y_psum"], g + 1)
                        dve.wait_ge(S["rms_ready"], g + 1)
                        dve.wait_ge(S["xb_ready"], g + 1)
                        row = view(xy, i * D, D)
                        v.scalar_tensor_tensor(row, ps[7][:, 0:D], rms[:, q:q + 1], row, ALU.mult, ALU.add).then_inc(S["y_ready"], 1)
                    i = t - 2
                    if live(i, CHUNKS):
                        g = b * CHUNKS + i
                        dve.wait_ge(S["o_moved"], 2 * g + 1)
                        dve.wait_ge(S["u_psum"], g + 1)
                        need(dve, S["y_psum"], g)
                        for n in range(KC):
                            v.scalar_tensor_tensor(zT[:, n * P:(n + 1) * P], ps[6][:, n * P:(n + 1) * P],
                                                   inv_p[:, :], oT[:, n * P:(n + 1) * P],
                                                   ALU.mult, ALU.mult).then_inc(S["z_ready"], 1)
                dve.wait_ge(S["state_psum"], (b + 1) * CHUNKS)
                steps(dve, CHUNKS, 0, 3, step_b)

            dve.wait_ge(S["o_psum"], TILES)
            for k in range(PIECES):
                hi, lo = piece_parts(k)
                dve.wait_ge(S["tot_ready"], k + 2)
                power(tot[:, k:k + 1], expo[:, k:k + 1], scale[:, k:k + 1], inv[:, k:k + 1], S["scale_ready"])
                dve.wait_ge(S["hi_ready"], k + 2)
                v.scalar_tensor_tensor(lo, stg[:, (k % 2) * WPIECE:(k % 2 + 1) * WPIECE], scale[:, k:k + 1], hi,
                                       ALU.mult, ALU.subtract).then_inc(S["lo_ready"], 1)
            b1_tot, h_tot, h_up, h_down, s1, s2 = (hsc[:, a * 8:(a + 1) * 8] for a in range(1, 7))
            h_e = expo[:, 0:EXPERTS]
            chain(v.tensor_tensor(b1_sq[:, :], b1_cols[:, :], b1_cols[:, :], ALU.mult))
            v.reduce_sum(hsc[:, 0:8], b1_sq[:, :].rearrange("p (e f) -> p e f", f=FC), AX.X).then_inc(S["b1_sum"], 2)
            dve.wait_ge(S["b1_tot"], 1)
            chain(v.scalar_tensor_tensor(h_tot, tot[:, 0:PIECES:2], float(D), b1_tot, ALU.mult, ALU.add))
            chain(v.tensor_scalar(h_tot, h_tot, 2.0, None, ALU.mult))
            power(h_tot, h_e, h_up, h_down)
            chain(v.tensor_tensor(s1, inv[:, 0:PIECES:2], h_up, ALU.mult))
            chain(v.tensor_scalar(s1, s1, 1.0 / XS, None, ALU.mult))
            chain(v.tensor_tensor(s2, inv[:, 1:PIECES:2], h_down, ALU.mult))
            b3 = b1_cols[:, :].rearrange("p (e f) -> p e f", f=FC)
            chain(v.tensor_tensor(b3, b3, h_up.rearrange("p (e a) -> p e a", a=1).broadcast_to([P, EXPERTS, FC]), ALU.mult))
            dve.wait_ge(S["b_late"], 16)

            def step(t, m):
                if live(t, SORTED):
                    k = m % 4
                    dve.wait_ge(S["xs_in"][m], 2 * (t - m) + 16)
                    need(dve, S["ye_out"][k], 4 * (t - k))
                    v.tensor_copy(ids[:, k:k + 1], moe_rows[m][:, D + 1:D + 2].bitcast(U32)).then_inc(S["ids_ready"], 1)
                    dve.wait_ge(S["moe_xhi"], t + 1)
                    v.scalar_tensor_tensor(moe_x[m % 2][:, D:2 * D], ps[0][:, 0:D], XS, moe_x[m % 2][:, 0:D],
                                           ALU.mult, ALU.subtract).then_inc(S["moe_xlo"], 1)
                i = t - 3
                if live(i, SORTED):
                    e = nc.vector.value_load(exp_of[0:1, bass.ds(i, 1)], min_val=0, max_val=EXPERTS - 1)
                    dve.wait_ge(S["ye_psum"], i + 1)
                    need(dve, S["ye_ready"], i)
                    v.scalar_tensor_tensor(moe_s, ps[3 + (m + 1) % 2][:, 0:D], view(s2, e, 1), view(b2_rows, e * D, D),
                                           ALU.mult, ALU.add).then_inc(S["y_summed"], 1)
                i = t - 1
                if live(i, SORTED):
                    e = nc.vector.value_load(exp_of[0:1, bass.ds(i, 1)], min_val=0, max_val=EXPERTS - 1)
                    for n in range(2):
                        dve.wait_ge(S["h_psum"], 2 * i + n + 1)
                        need(dve, S["hlo_ready"], 2 * i)
                        bias = view(b1_cols, e * FC + 4 * n, 4).rearrange("p (f a) -> p f a", a=1).broadcast_to([P, 4, P])
                        v.scalar_tensor_tensor(moe_h[:, n * 512:(n + 1) * 512].rearrange("p (f n) -> p f n", f=4),
                                               ps[1 + n][:, :].rearrange("p (f n) -> p f n", f=4), view(s1, e, 1), bias,
                                               ALU.mult, ALU.add).then_inc(S["h_ready"], 1)
                    for n in range(2):
                        dve.wait_ge(S["hhi_ready"], 2 * i + n + 1)
                        hh = moe_hh[(m - 1) % 2]
                        v.scalar_tensor_tensor(hh[:, 1024 + n * 512:1024 + (n + 1) * 512], moe_h[:, n * 512:(n + 1) * 512], 0.0,
                                               hh[:, n * 512:(n + 1) * 512], ALU.max, ALU.subtract).then_inc(S["hlo_ready"], 1)
            moe_steps(dve, 3, step)

        @block.tensor
        def _(pe):
            mm = nc.tensor.matmul
            pe.wait_ge(S["gp_const"], 8)
            pe.wait_ge(S["const_in"], 80)
            pe.wait_ge(S["bias_t"], 7)
            pe.wait_ge(S["scale_ready"], 2)
            pe.wait_ge(S["lo_ready"], 1)

            def split_mm(dst, pairs, first, last):
                n = 0
                for (sh, sl), (mh, ml) in pairs:
                    for s, m in ((sh, mh), (sl, mh), (sh, ml)):
                        ins = mm(dst, s, m, start=first and n == 0, stop=last and n == 3 * len(pairs) - 1)
                        n += 1
                return ins

            def xpair(off, k):
                x16 = view(ring, off, D).bitcast(F16)
                return x16[:, k * P:(k + 1) * P], x16[:, D + k * P:D + (k + 1) * P]

            def wpair(k, lo, cols):
                return w_hi[:, k * PCOLS + lo:k * PCOLS + lo + cols], w_lo[:, k * PCOLS + lo:k * PCOLS + lo + cols]

            for b in range(BATCH):
                def step_a(t, par, b=b):
                    if live(t, CHUNKS):
                        g = b * CHUNKS + t
                        pe.wait_ge(S["xn_ready"], g + 1)
                        need(pe, S["xlo_ready"], g)
                        for k in range(KC):
                            ins = nc.tensor.transpose(ps[0][:, k * P:(k + 1) * P], xn[:, par * D + k * P:par * D + (k + 1) * P], ident[:, :])
                        ins.then_inc(S["xT_psum"], 1)
                    i = t - 1
                    if live(i, CHUNKS):
                        g = b * CHUNKS + i
                        pe.wait_ge(S["xlo_ready"], g + 1)
                        need(pe, S["lg_ready"], g)
                        mm(ps[1][:, :], ones_s[:, :], bias_p[:, 0:512], start=True, stop=False)
                        split_mm(ps[1][:, :], [(xpair(i * SLOT + 768, k), wpair(k, KV, 512)) for k in range(KC)], False, True)
                        split_mm(ps[2][:, 0:EXPERTS], [(xpair(i * SLOT + 768, k), wpair(k, RT, EXPERTS)) for k in range(KC)],
                                 True, True).then_inc(S["kv_psum"], 1)
                    i = t - 2
                    if live(i, CHUNKS):
                        g = b * CHUNKS + i
                        pe.wait_ge(S["rope_k"], 2 * g + 2)
                        need(pe, S["kT_ready"], g)
                        for a in range(4):
                            ins = nc.tensor.transpose(ps[3][:, a * P:(a + 1) * P], rot[:, par * 512 + a * P:par * 512 + (a + 1) * P], ident[:, :])
                        ins.then_inc(S["kT_psum"], 1)
                        pe.wait_ge(S["v_ready"], g + 1)
                        need(pe, S["state_ready"], 2 * g)
                        for a in range(4):
                            ins = mm(ps[4][:, a * P:(a + 1) * P], rot[:, par * 512 + a * P:par * 512 + (a + 1) * P],
                                     view(ring, i * SLOT + 512 + (a // 2) * P, P), start=True, stop=True)
                        ins.then_inc(S["state_psum"], 1)
                if b:
                    pe.wait_ge(S["q_moved"], 3 * b * CHUNKS)
                    pe.wait_ge(S["q_act"], b * CHUNKS)
                    pe.wait_ge(S["s_masked"], 2 * b * CHUNKS)
                steps(pe, CHUNKS, 0, 2, step_a)
                if b == BATCH - 1:
                    pe.wait_ge(S["kT_ready"], TILES)
                    pe.wait_ge(S["state_ready"], 2 * TILES)
                    pe.wait_ge(S["route_a"], 7)
                    mm(ps[3][:, 0:256], upper[:, :], small[:, 872:1128], start=True, stop=True).then_inc(S["route_pe"], 1)
                    mm(ps[4][:, 0:256], ones[:, :], small[:, 872:1128], start=True, stop=True).then_inc(S["route_pe"], 1)
                    pe.wait_ge(S["route_b"], 3)

                def step_b(t, par, b=b):
                    i = t - 1
                    q = 1 - par
                    if live(i, CHUNKS):
                        g = b * CHUNKS + i
                        pe.wait_ge(S["rope_q"], 2 * g + 2)
                        need(pe, S["q_moved"], 3 * g)
                        for a in range(4):
                            ins = nc.tensor.transpose(ps[0][:, a * P:(a + 1) * P], rot[:, q * 512 + a * P:q * 512 + (a + 1) * P], ident[:, :])
                        ins.then_inc(S["qT_psum"], 1)
                    if live(t, CHUNKS):
                        g = b * CHUNKS + t
                        need(pe, S["q_act"], g - 1)
                        mm(ps[1 + par][:, 0:D], ones_s[:, :], bias_p[:, 512:768], start=True, stop=False)
                        split_mm(ps[1 + par][:, 0:D], [(xpair(t * SLOT + 768, k), wpair(k, Q, D)) for k in range(KC)],
                                 False, True).then_inc(S["q_psum"], 1)
                    if live(i, CHUNKS):
                        g = b * CHUNKS + i
                        pe.wait_ge(S["q_moved"], 3 * g + 2)
                        pe.wait_ge(S["k_now"], 16 * g + 16)
                        for n in range(2):
                            need(pe, S["s_masked"], 2 * g - 1 + n)
                            for a in range(2):
                                pair = 2 * n + a
                                ins = mm(ps[3 + n][:, a * D:(a + 1) * D], kT_now[:, pair * P:(pair + 1) * P],
                                         qbd[:, pair * D:(pair + 1) * D], start=True, stop=True)
                            ins.then_inc(S["s_psum"], 1)
                    i = t - 3
                    if live(i, CHUNKS):
                        g = b * CHUNKS + i
                        pe.wait_ge(S["z_ready"], 2 * g + 2)
                        pe.wait_ge(S["o_moved"], 2 * g + 2)
                        for k in range(KC):
                            ins = mm(ps[6][:, D:D + 96], osq[:, k * P:(k + 1) * P], ones[:, 0:96],
                                     start=k == 0, stop=k == KC - 1)
                        ins.then_inc(S["ms_psum"], 1)
                        need(pe, S["y_ready"], g)
                        for k in range(KC):
                            ins = mm(ps[7][:, 0:D], zT[:, k * P:(k + 1) * P], wo_sb[:, k * D:(k + 1) * D],
                                     start=k == 0, stop=k == KC - 1)
                        ins.then_inc(S["y_psum"], 1)
                    i = t - 2
                    if live(i, CHUNKS):
                        g = b * CHUNKS + i
                        need(pe, S["z_ready"], 2 * g)
                        need(pe, S["ms_ready"], g)
                        for n in range(KC):
                            mm(ps[6][:, n * P:(n + 1) * P], bias_p[:, 768 + n * P:768 + (n + 1) * P], ones_s[:, :], start=True, stop=False)
                            ins = split_mm(ps[6][:, n * P:(n + 1) * P],
                                           [(wpair(k, U + n * P, P), xpair(i * SLOT + 768, k)) for k in range(KC)], False, True)
                        ins.then_inc(S["u_psum"], 1)
                        pe.wait_ge(S["v_now"], 16 * g + 16)
                        pe.wait_ge(S["w_ready"], g + 1)
                        need(pe, S["o_moved"], 2 * g)
                        pe.wait_ge(S["q_moved"], 3 * g + 3)
                        pe.wait_ge(S["s_masked"], 2 * g + 2)
                        for n in range(2):
                            for a in range(2):
                                pair = 2 * n + a
                                mm(ps[5][64 * a:64 * a + 64, n * P:(n + 1) * P], w_now[:, par * D + pair * 64:par * D + (pair + 1) * 64],
                                   qT[:, par * 512 + pair * P:par * 512 + (pair + 1) * P], start=True, stop=False, skip_group_check=True)
                            for hh in range(4):
                                h = 4 * n + hh
                                ins = mm(ps[5][32 * hh:32 * hh + 32, n * P:(n + 1) * P], v_now[:, h * HD:(h + 1) * HD],
                                         masked[:, par * 1024 + h * P:par * 1024 + (h + 1) * P], start=False, stop=True,
                                         skip_group_check=True)
                        ins.then_inc(S["o_psum"], 1)
                pe.wait_ge(S["lg_ready"], (b + 1) * CHUNKS)
                pe.wait_ge(S["kT_ready"], (b + 1) * CHUNKS)
                pe.wait_ge(S["state_ready"], 2 * (b + 1) * CHUNKS)
                steps(pe, CHUNKS, 0, 3, step_b)

            pe.wait_ge(S["lo_ready"], 1 + PIECES)
            pe.wait_ge(S["y_ready"], TILES)

            def step(t, m):
                if live(t, SORTED):
                    pe.wait_ge(S["xs_in"][m], 2 * (t - m) + 16)
                    need(pe, S["moe_xlo"], t)
                    for k in range(KC):
                        ins = nc.tensor.transpose(ps[0][:, k * P:(k + 1) * P], moe_rows[m][:, k * P:(k + 1) * P], ident[:, :])
                    ins.then_inc(S["xt_psum"], 1)
                i = t - 1
                if live(i, SORTED):
                    e = nc.tensor.value_load(exp_of[0:1, bass.ds(i, 1)], min_val=0, max_val=EXPERTS - 1)
                    r16 = region[:, :].bitcast(F16)
                    xh = moe_x[(m - 1) % 2]
                    pe.wait_ge(S["moe_xlo"], i + 1)
                    for n in range(2):
                        need(pe, S["h_ready"], 2 * i - 1 + n)
                        for f in range(4):
                            col = (4 * n + f) * P
                            pairs = [((view(r16, e * 4 * WPIECE + k * FF + col, P), view(r16, e * 4 * WPIECE + WPIECE + k * FF + col, P)),
                                      (xh[:, k * P:(k + 1) * P], xh[:, D + k * P:D + (k + 1) * P])) for k in range(KC)]
                            ins = split_mm(ps[1 + n][:, f * P:(f + 1) * P], pairs, True, True)
                        ins.then_inc(S["h_psum"], 1)
                i = t - 2
                if live(i, SORTED):
                    e = nc.tensor.value_load(exp_of[0:1, bass.ds(i, 1)], min_val=0, max_val=EXPERTS - 1)
                    r16 = region[:, :].bitcast(F16)
                    hh = moe_hh[m % 2]
                    need(pe, S["y_summed"], i - 1)
                    pe.wait_ge(S["hlo_ready"], 2 * i + 2)
                    pairs = [((hh[:, f * P:(f + 1) * P], hh[:, 1024 + f * P:1024 + (f + 1) * P]),
                              (view(r16, (e * 4 + 2) * WPIECE + f * D, D), view(r16, (e * 4 + 3) * WPIECE + f * D, D)))
                             for f in range(FC)]
                    split_mm(ps[3 + m % 2][:, 0:D], pairs, True, True).then_inc(S["ye_psum"], 1)
            moe_steps(pe, 2, step)


def kernel(**inputs):
    import concourse.bacc as bacc
    from concourse.bass_utils import run_bass_kernel_spmd

    g = {n: np.asarray(a) for n, a in inputs.items()}
    wt = g["L0_attn_qkvu_w"].T
    q, k, v, u = (wt[:, n * D:(n + 1) * D] for n in range(4))
    proj = np.concatenate([k, v, g["L0_ffn_w_router"], q, u], axis=1)
    bq, bk, bv, bu = (g["L0_attn_qkvu_b"][n * D:(n + 1) * D] for n in range(4))

    def rows(w, chunks):
        return w.reshape(chunks, P, -1).transpose(1, 0, 2).reshape(P, -1)

    w1 = g["L0_ffn_w1"].reshape(EXPERTS, KC, P, FF).transpose(2, 0, 1, 3).reshape(P, EXPERTS, WPIECE)
    w2 = g["L0_ffn_w2"].reshape(EXPERTS, FC, P, D).transpose(2, 0, 1, 3).reshape(P, EXPERTS, WPIECE)
    arrays = {
        "x": g["L0_attn_x"].reshape(-1, D), "slope": g["L0_attn_slope_rate"].reshape(1, HEADS),
        "wqkvu": rows(proj, KC), "bqkvu": np.concatenate([bk, bv, bq, bu])[None], "wout": rows(g["L0_attn_out_w"].T, KC),
        "bout": g["L0_attn_out_b"][None], "theta": g["L0_attn_theta"].reshape(1, D),
        "wexp": np.stack([w1, w2], axis=2).reshape(P, -1),
        "b1": g["L0_ffn_b1"].reshape(EXPERTS, FC, P).transpose(2, 0, 1).reshape(P, -1),
        "b2": g["L0_ffn_b2"].reshape(1, -1),
    }
    arrays = {n: np.ascontiguousarray(a) for n, a in arrays.items()}
    nc = bacc.Bacc("TRN2", target_bir_lowering=False, num_devices=1)
    args = [nc.dram_tensor(n, a.shape, mybir.dt.from_np(a.dtype), kind="ExternalInput").ap() for n, a in arrays.items()]
    out = nc.dram_tensor("out", (TILES * P, D), F32, kind="ExternalOutput").ap()
    xn_d = nc.dram_tensor("xn_rows", (TILES * P, D), F32).ap()
    sorted_d = nc.dram_tensor("sorted_rows", (SORTED * P, ROW), F32).ap()
    build(nc, *args, out, xn_d, sorted_d)
    r = run_bass_kernel_spmd(nc, [arrays], core_ids=[0])
    return r.results[0]["out"].reshape(BATCH, SEQ, D)
```

```python
from contextlib import ExitStack

import numpy as np
import concourse.bass as bass
from concourse import mybir

F32 = mybir.dt.float32
F16 = mybir.dt.float16
BF16 = mybir.dt.bfloat16
I32 = mybir.dt.int32
U32 = mybir.dt.uint32
ALU = mybir.AluOpType
ACT = mybir.ActivationFunctionType
AX = mybir.AxisListType

P = 128
BATCH, SEQ, D = 2, 2048, 256
HEADS, HD = 8, 32
EXPERTS, FF = 8, 1024
KC = D // P
CHUNKS = SEQ // P
TILES = BATCH * CHUNKS
FC = FF // P
SORTED = TILES + EXPERTS - 1
ROW = D + 2
NOBODY = 1 << 20
LN_EPS = 1e-5
RMS_EPS = 1e-6
TWO_PI_A = 6.28125
TWO_PI_B = float(2 * np.pi - TWO_PI_A)
ROUND = 1.5 * 2.0 ** 23
PI_IN = 3.1415925
WPIECE = 2048
PIECES = 2 * EXPERTS
KV, RT, Q, U = 0, 512, 520, 776
PCOLS = 4 * D + EXPERTS
XS = 256.0
SLOT = 1792
V_AT, X_AT, COS_AT, SIN_AT, STATE_AT = 512, 768, 1024, 1280, 1536
PEEL = 6
MOE_PEEL = 7
MOE_ROWS = 8
PADS = SORTED - TILES
DISPATCH_STEP = 4
assert TILES == 2 * CHUNKS
PIECE_STEP = {k: min(-(-(k + 1) * WPIECE // SLOT), CHUNKS) + 1 for k in range(PIECES - 2)}


def rows_of(step):
    return range(2 * (step - DISPATCH_STEP), 2 * (step - DISPATCH_STEP) + 2)


def pieces_of(b, step):
    return [k for k in PIECE_STEP if b == BATCH - 1 and PIECE_STEP[k] == step]


def need(engine, sem, count):
    if not isinstance(count, int) or count > 0:
        engine.wait_ge(sem, count)


def live(t, n):
    return not isinstance(t, int) or 0 <= t < n


def steps(eng, n, lead, lag, step):
    pairs = (n - lead - PEEL) // 2
    for t in range(-lead, PEEL):
        step(t, t & 1)
    with eng.Fori(0, pairs) as k:
        step(k * 2 + PEEL, 0)
        step(k * 2 + PEEL + 1, 1)
    for t in range(PEEL + 2 * pairs, n + lag):
        step(t, t & 1)


def moe_steps(eng, lag, step, begin=None):
    assert (SORTED - MOE_PEEL) % MOE_ROWS == 0
    for t in range(MOE_PEEL):
        step(t, t)
    with eng.Fori(0, (SORTED - MOE_PEEL) // MOE_ROWS) as k:
        if begin:
            begin(k * MOE_ROWS + MOE_PEEL, MOE_PEEL)
        for u in range(MOE_ROWS):
            step(k * MOE_ROWS + MOE_PEEL + u, (MOE_PEEL + u) % MOE_ROWS)
    if begin:
        begin(SORTED, SORTED % MOE_ROWS)
    for t in range(SORTED, SORTED + lag):
        step(t, t % MOE_ROWS)


def view(t, off, cols):
    return t[:, bass.ds(off, cols)]


def build(nc, x, slope, wqkvu, bqkvu, wout, bout, theta, wexp, b1, b2, out, xn_d, sorted_d):
    ctx = ExitStack()
    with ctx:
        def sb(name, cols, dt=F32):
            return ctx.enter_context(nc.sbuf_tensor(name, [P, cols], dt))

        region = sb("region", PIECES * WPIECE)
        at = [0]

        def part(cols):
            at[0] += cols
            return region[:, at[0] - cols:at[0]]

        ring = part(CHUNKS * SLOT)
        qT = part(2 * 512)
        kT_now = part(512)
        assert at[0] == CHUNKS * SLOT + STATE_AT
        angle_now, size_now = ([qT[:, (2 * a + k) * D:(2 * a + k + 1) * D] for k in range(2)] for a in range(2))
        turns = kT_now[:, 0:D]
        final_state = part(D)
        masked = part(2 * HEADS * P)
        v_now = part(D)
        slots = region[:, 0:(CHUNKS + 1) * SLOT].rearrange("p (c w) -> p c w", w=SLOT)

        def state(c):
            return region[:, bass.ds(c * SLOT + STATE_AT, D)]

        assert at[0] <= PIECES * WPIECE

        xy = sb("xy", CHUNKS * D)
        stg = sb("stg", 2 * WPIECE)
        work = sb("work", 5392)
        w_hi = work[:, 0:1032].bitcast(F16)
        w_lo = work[:, 1032:2064].bitcast(F16)
        wo_sb, mask, rot, w_now, w_term = (work[:, a:b] for a, b in (
            (2064, 2576), (2576, 3600), (3600, 4624), (4624, 5136), (5136, 5392)))
        act_k, oT, osq, zT = (sb(name, cols)[:, :] for name, cols in (("act_k", 512), ("oT", D), ("osq", D), ("zT", D)))
        spare = sb("spare", WPIECE)
        xn = spare[:, 0:512]
        bias_room = stg[0:4 * D // P, 2 * PCOLS + D:2 * PCOLS + D + 4 * P]
        bias_f = bias_room[:, 0:P]
        bias_part = [bias_room[:, P * (q + 1):P * (q + 1) + P // 2].bitcast(BF16) for q in range(3)]
        qbd = sb("qbd", 1024)
        row_bufs = [work[:, k * PCOLS // 2:k * PCOLS // 2 + ROW] for k in range(4)]
        assert 2 * ROW <= Q
        theta_row = stg[:, 2 * PCOLS:2 * PCOLS + D]
        moe_x = [work[:, k * D:(k + 1) * D].bitcast(F16) for k in range(2)]
        moe_h = work[:, 512:1536]
        moe_hh = [work[:, 1536 + k * 1024:2560 + k * 1024].bitcast(F16) for k in range(2)]
        moe_y = [work[:, 3584 + k * D:3840 + k * D] for k in range(4)]
        moe_s = work[:, 4608:4608 + D]
        moe_rows = [xy[:, CHUNKS * D - (k + 1) * ROW:CHUNKS * D - k * ROW] for k in range(MOE_ROWS)]
        moe_h_rows = xy[:, 0:FF]
        b2_rows = stg[:, WPIECE:WPIECE + EXPERTS * D]

        es_row = sb("es_row", D)
        pad_row = sb("pad_row", ROW)
        bout_row = pad_row[:, 0:D]
        ident = sb("ident", P)
        ones = sb("ones", P)
        upper = sb("upper", P)
        ones_s = sb("ones_s", P, BF16)
        bias_p = sb("bias_p", 4 * D, BF16)
        neghalf = sb("neghalf", 1)
        halfpi = sb("halfpi", 1)
        st6 = sb("st6", 12)
        mv = sb("mv", 4)
        vare = sb("vare", 2)
        rstd = sb("rstd", 2)
        mse = sb("mse", 2)
        rms = sb("rms", 2)
        slope_bc = sb("slope_bc", HEADS)
        es = sb("es", HEADS)
        pos0 = sb("pos0", CHUNKS)
        logits = sb("logits", TILES * EXPERTS)
        posi = sb("posi", TILES, U32)
        pad_posi = sb("pad_posi", PADS, U32)
        starts = sb("starts", SORTED)
        exp_of = sb("exp_of", SORTED, I32)
        tag = sb("tag", 2 * TILES)
        ini = sb("ini", SORTED, I32)
        ids = sb("ids", 4, U32)
        ssq = sb("ssq", PIECES + 1)
        tot = sb("tot", PIECES + 1)
        expo = sb("expo", PIECES + 1, I32)
        scale = sb("scale", PIECES + 1)
        inv = sb("inv", PIECES + 1)
        inv_p = sb("inv_p", 1)
        b1_cols = sb("b1_cols", EXPERTS * FC)
        b1_sq = osq[:, 0:EXPERTS * FC]
        hsc = sb("hsc", 8 * EXPERTS)

        ps = [ctx.enter_context(nc.psum_tensor(f"bank{i}", [P, 512], F32)) for i in range(8)]

        xT_bank, kv_bank, lg_bank = (ps[0], ps[5]), (ps[1], ps[6]), (ps[2], ps[7])

        S = {}
        for n in """theta_in const_in wp_in xn_ready xT_psum xhi_ready xlo_ready kv_psum k_act v_ready lg_ready rope_k
            kT_psum kT_ready k_now v_now state_psum state_ready stat var_ready rstd_ready pad_set pad_out q_psum q_act rope_q qT_psum
            q_moved s_psum s_masked w_part w_ready u_psum o_psum o_moved z_ready ms_psum ms_ready rms_ready xb_ready
            y_psum y_ready gp_const angle tab sines mask_part rows bias_t bias_in es_ready
            route_a pad_step route_act route_pe route_b disp_tag ssq_ready tot_ready scale_step scale_ready hi_ready lo_ready
            b_late b1_sum b1_tot xt_psum moe_xhi moe_xlo h_rows_psum h_rows_ready h_psum h_ready hhi_ready hlo_ready
            ye_psum y_summed ye_ready
            ids_ready""".split():
            S[n] = ctx.enter_context(nc.semaphore(n))
        for n, k in (("x_in", 2), ("xn_out", 2), ("row_out", 2), ("disp_in", 4), ("disp_out", 4), ("w_in", 3),
                     ("xs_in", MOE_ROWS), ("ye_out", 4)):
            S[n] = [ctx.enter_context(nc.semaphore(f"{n}{i}")) for i in range(k)]

        block = ctx.enter_context(nc.Block())

        def piece_in(k):
            return spare[:, :] if k % 3 == 2 else stg[:, (k % 3) * WPIECE:(k % 3 + 1) * WPIECE]

        def piece_parts(k):
            p = region[:, k * WPIECE:(k + 1) * WPIECE].bitcast(F16)
            return p[:, 0:WPIECE], p[:, WPIECE:2 * WPIECE]

        @block.sync
        def _(sp):
            sp.dma_start(stg[:, 0:2 * PCOLS], wqkvu).then_inc(S["wp_in"], 16)

            def load_x(b, i, par):
                if live(i, CHUNKS):
                    g = b * CHUNKS + i
                    need(sp, S["x_in"][par], 8 * (g - par))
                    if b:
                        sp.wait_ge(S["row_out"][par], 8 * (i - par) + 16)
                    sp.dma_start(view(xy, i * D, D), x[bass.ds(g * P, P), :]).then_inc(S["x_in"][par], 16)

            def load_piece(k):
                if k == 2:
                    sp.wait_ge(S["route_b"], 3)
                sp.wait_ge(S["lo_ready"], max(k - 1, 1))
                sp.wait_ge(S["hi_ready"], max(k - 1, 1))
                sp.dma_start(piece_in(k), wexp[:, k * WPIECE:(k + 1) * WPIECE]).then_inc(S["w_in"][k % 3], 16)

            for b in range(BATCH):
                def step_a(t, par, b=b):
                    if not (b and isinstance(t, int) and t < 0):
                        load_x(b, t + 4, par)
                    if live(t, CHUNKS):
                        g = b * CHUNKS + t
                        sp.wait_ge(S["xn_ready"], g + 1)
                        sp.dma_start(xn_d[bass.ds(g * P, P), :], xn[:, par * D:(par + 1) * D]).then_inc(S["xn_out"][par], 16)
                steps(sp, CHUNKS, 4, 0, step_a)

                def step_b(t, par, b=b):
                    if b < BATCH - 1 and isinstance(t, int) and t >= CHUNKS:
                        load_x(b + 1, t - CHUNKS, par)
                    i = t - 1
                    if live(i, CHUNKS):
                        g = b * CHUNKS + i
                        need(sp, S["o_psum"], g)
                        sp.dma_start(v_now, view(ring, i * SLOT + V_AT, D)).then_inc(S["v_now"], 16)
                    for k in pieces_of(b, t - 2):
                        if k + 3 < PIECES:
                            load_piece(k + 3)
                    i = t - 4
                    if live(i, CHUNKS):
                        g = b * CHUNKS + i
                        sp.wait_ge(S["y_ready"], g + 1)
                        need(sp, S["row_out"][par], 8 * (g - par))
                        sp.dma_start(out[bass.ds(g * P, P), :], view(xy, i * D, D)).then_inc(S["row_out"][par], 16)
                    if live(t, CHUNKS):
                        g = b * CHUNKS + t
                        need(sp, S["s_psum"], 2 * g)
                        sp.wait_ge(S["kT_ready"], (b + 1) * CHUNKS)
                        sp.dma_start(kT_now, view(ring, t * SLOT, 512)).then_inc(S["k_now"], 16)
                sp.wait_ge(S["v_ready"], (b + 1) * CHUNKS)
                if b < BATCH - 1:
                    steps(sp, CHUNKS, 0, 4, step_b)
                else:
                    load_piece(0)
                    load_piece(1)
                    for t in range(CHUNKS + 4):
                        step_b(t, t & 1)
                        if t == DISPATCH_STEP:
                            load_piece(2)



            for slot in range(4):
                sp.wait_ge(S["disp_out"][slot], 16 * TILES // 4)
            sp.wait_ge(S["pad_out"], 16 * PADS)
            for q in range(2):
                sp.wait_ge(S["row_out"][q], 8 * TILES)

            def load_sorted(t, slot):
                need(sp, S["ye_ready"], t - 6)
                need(sp, S["ids_ready"], t - 6)
                sp.dma_start(moe_rows[slot], sorted_d[bass.ds(t * P, P), :]).then_inc(S["xs_in"][slot], 16)
            moe_steps(sp, 0, load_sorted)

        @block.gpsimd
        def _(gp):
            K = S["gp_const"]
            gp.iota(ini[:, 0:CHUNKS], [[P, CHUNKS]], base=0, channel_multiplier=1).then_inc(K, 1)
            gp.wait_ge(K, 1)
            gp.tensor_copy(pos0[:, :], ini[:, 0:CHUNKS]).then_inc(K, 1)
            gp.memset(halfpi[:, :], float(np.pi / 2)).then_inc(K, 1)
            gp.memset(ident[:, :], 0.0).then_inc(K, 1)
            gp.memset(ones[:, :], 1.0).then_inc(K, 1)
            gp.memset(neghalf[:, :], -0.5).then_inc(K, 1)
            gp.wait_ge(K, 6)
            gp.affine_select(out=ident[:, :], in_=ident[:, :], compare_op=ALU.not_equal, fill=1.0,
                             base=0, pattern=[[-1, P]], channel_multiplier=1).then_inc(K, 1)
            gp.affine_select(out=upper[:, :], in_=ones[:, :], compare_op=ALU.is_gt, fill=0.0,
                             base=0, pattern=[[1, P]], channel_multiplier=-1).then_inc(K, 1)
            gp.wait_ge(K, 8)
            gp.memset(slots[:, :, STATE_AT:STATE_AT + D], 0.0).then_inc(K, 1)
            B = S["bias_t"]
            gp.memset(bias_p[:, :], 0.0).then_inc(B, 1)
            gp.wait_ge(S["bias_in"], 16)
            gp.tensor_copy(bias_part[0], bias_f).then_inc(B, 1)
            gp.wait_ge(B, 2)
            gp.tensor_tensor(bias_f, bias_f, bias_part[0], ALU.subtract).then_inc(B, 1)
            gp.wait_ge(B, 3)
            gp.tensor_copy(bias_part[1], bias_f).then_inc(B, 1)
            gp.wait_ge(B, 4)
            gp.tensor_tensor(bias_f, bias_f, bias_part[1], ALU.subtract).then_inc(B, 1)
            gp.wait_ge(B, 5)
            gp.tensor_copy(bias_part[2], bias_f).then_inc(B, 1)
            gp.wait_ge(S["ssq_ready"], 1)
            gp.partition_all_reduce(tot[:, PIECES:PIECES + 1], ssq[:, PIECES:PIECES + 1], P, bass.bass_isa.ReduceOp.add).then_inc(S["tot_ready"], 1)

            def angles(c):
                gp.tensor_scalar(view(ring, c * SLOT + SIN_AT, D), theta_row, view(pos0, c, 1), None, ALU.mult).then_inc(S["angle"], 1)

            gp.wait_ge(S["theta_in"], 16)
            angles(0)

            def deviation(b, t, par):
                g = b * CHUNKS + t
                need(gp, S["xn_ready"], g - 1)
                gp.wait_ge(S["var_ready"], g + 1)
                gp.tensor_tensor(rstd[:, par:par + 1], vare[:, par:par + 1], neghalf[:, :], ALU.pow).then_inc(S["rstd_ready"], 1)

            deviation(0, 0, 0)
            deviation(0, 1, 1)
            angles(1)
            for t in range(2, CHUNKS):
                deviation(0, t, t & 1)
                angles(t)
            gp.memset(qbd[:, :], 0.0).then_inc(K, 1)
            gp.iota(tag[:, :].bitcast(I32).rearrange("p (t c) -> p t c", c=2)[:, :, 1:2], [[P, TILES], [0, 1]], base=0,
                    channel_multiplier=1).then_inc(K, 1)
            gp.iota(ini[:, :], [[P, SORTED]], base=0, channel_multiplier=0).then_inc(K, 1)
            gp.wait_ge(K, 12)
            gp.tensor_copy(starts[:, :], ini[:, :]).then_inc(K, 1)
            gp.memset(pad_row[:, D:D + 1], 0.0).then_inc(S["pad_set"], 1)
            gp.memset(pad_row[:, D + 1:D + 2].bitcast(I32), NOBODY).then_inc(S["pad_set"], 1)

            gp.wait_ge(S["b1_sum"], 2)
            gp.partition_all_reduce(hsc[:, 8:16], hsc[:, 0:8], P, bass.bass_isa.ReduceOp.add).then_inc(S["b1_tot"], 1)

            def sum_piece(k):
                gp.wait_ge(S["ssq_ready"], k + 2)
                gp.partition_all_reduce(tot[:, k:k + 1], ssq[:, k:k + 1], P, bass.bass_isa.ReduceOp.add).then_inc(S["tot_ready"], 1)

            for b in range(BATCH):
                if b:
                    for t in range(4):
                        deviation(b, t, t & 1)
                    with gp.Fori(0, (CHUNKS - 4) // 2) as k:
                        deviation(b, k * 2 + 4, 0)
                        deviation(b, k * 2 + 5, 1)

                def step_b(t, par, b=b):
                    for k in pieces_of(b, t - 1):
                        sum_piece(k)
                    i = t - 1
                    if live(i, CHUNKS):
                        g = b * CHUNKS + i
                        w = w_now[:, (1 - par) * D:(2 - par) * D]
                        need(gp, S["o_psum"], g - 1)
                        need(gp, S["w_ready"], g)
                        gp.tensor_tensor(w, final_state, state(i + 1),
                                         ALU.subtract).then_inc(S["w_part"], 1)
                        gp.tensor_tensor(w_term, state(i), es_row[:, :], ALU.mult).then_inc(S["w_part"], 1)
                        gp.wait_ge(S["w_part"], 2 * g + 2)
                        gp.tensor_tensor(w, w, w_term, ALU.add).then_inc(S["w_ready"], 1)
                    if live(t, CHUNKS):
                        gp.tensor_tensor(view(xy, t * D, D), view(xy, t * D, D), bout_row, ALU.add).then_inc(S["xb_ready"], 1)
                    i = t - 3
                    if live(i, CHUNKS):
                        g = b * CHUNKS + i
                        q = 1 - par
                        need(gp, S["y_ready"], g - 1)
                        gp.wait_ge(S["ms_ready"], g + 1)
                        gp.tensor_tensor(rms[:, q:q + 1], mse[:, q:q + 1], neghalf[:, :], ALU.pow).then_inc(S["rms_ready"], 1)
                    if b == BATCH - 1 and t >= DISPATCH_STEP:
                        if t == DISPATCH_STEP:
                            gp.wait_ge(S["route_b"], 3)
                        for r in rows_of(t):
                            dst = row_bufs[r % 4]
                            gp.wait_ge(S["disp_in"][r % 4], 16 * (r // 4 + 1))
                            gp.tensor_copy(dst[:, D:D + 2].bitcast(U32), tag[:, 2 * r:2 * r + 2].bitcast(U32)).then_inc(S["disp_tag"], 1)
                            gp.wait_ge(S["disp_tag"], r + 1)
                            gp.indirect_dma_start(sorted_d[:, :], bass.IndirectOffsetOnAxis(ap=posi[:, r:r + 1], axis=0),
                                                  dst, None).then_inc(S["disp_out"][r % 4], 16)
                        n = t - DISPATCH_STEP
                        if n < PADS:
                            gp.wait_ge(S["pad_set"], 2)
                            gp.indirect_dma_start(sorted_d[:, :], bass.IndirectOffsetOnAxis(ap=pad_posi[:, n:n + 1], axis=0),
                                                  pad_row[:, :], None).then_inc(S["pad_out"], 16)
                gp.wait_ge(S["state_ready"], 2 * (b + 1) * CHUNKS)
                gp.wait_ge(S["rows"], 2)
                gp.wait_ge(S["const_in"], 64)
                if b < BATCH - 1:
                    steps(gp, CHUNKS, 0, 3, step_b)
                else:
                    for t in range(CHUNKS + DISPATCH_STEP):
                        if t == CHUNKS + DISPATCH_STEP - 1:
                            for k in range(PIECES - 2, PIECES):
                                sum_piece(k)
                        step_b(t, t & 1)

            for q in range(2):
                gp.wait_ge(S["row_out"][q], 8 * TILES)
            last_row = gp.to_reg(TILES * P - 1)
            for t in range(SORTED):
                slot = t % 4
                gp.wait_ge(S["ye_ready"], t + 1)
                gp.wait_ge(S["ids_ready"], t + 1)
                gp.indirect_dma_start(out[:, :], bass.IndirectOffsetOnAxis(ap=ids[:, slot:slot + 1], axis=0),
                                      moe_y[slot], None, bounds_check=last_row, oob_is_err=False,
                                      compute_op=ALU.add).then_inc(S["ye_out"][slot], 16)
            for slot in range(4):
                gp.wait_ge(S["ye_out"][slot], 16 * len(range(slot, SORTED, 4)))

        @block.scalar
        def _(act):
            C = S["const_in"]
            act.dma_start(theta_row, theta[0:1, :].broadcast_to([P, D])).then_inc(S["theta_in"], 16)
            act.dma_start(bias_f, bqkvu).then_inc(S["bias_in"], 16)
            act.dma_start(slope_bc[:, :], slope[0:1, :].broadcast_to([P, HEADS])).then_inc(C, 16)
            act.dma_start(wo_sb, wout).then_inc(C, 16)
            act.dma_start(bout_row, bout[0:1, :].broadcast_to([P, D])).then_inc(C, 16)
            act.dma_start(b1_cols[:, :], b1).then_inc(C, 16)
            act.wait_ge(C, 64)
            act.activation(es[:, :], slope_bc[:, :], ACT.Exp).then_inc(S["es_ready"], 1)
            act.wait_ge(S["es_ready"], 1)
            act.activation(hsc[:, 0:EXPERTS], es[:, :], ACT.Silu).then_inc(S["es_ready"], 1)
            act.wait_ge(S["wp_in"], 16)
            act.activation(w_hi, stg[:, 0:2 * PCOLS], ACT.Square, accum_out=ssq[:, PIECES:PIECES + 1]).then_inc(S["ssq_ready"], 1)
            act.wait_ge(S["bias_t"], 6)
            for q in range(3):
                act.dma_start(bias_p[32 * q:32 * q + 1, :], bias_part[q]).then_inc(S["bias_in"], 16)
            act.wait_ge(S["scale_ready"], 1)
            act.activation(w_hi, stg[:, 0:2 * PCOLS], ACT.Copy, scale=scale[:, PIECES:PIECES + 1]).then_inc(S["hi_ready"], 1)
            act.wait_ge(S["gp_const"], 3)

            def sines(c, par):
                r, size = angle_now[par], size_now[par]
                act.wait_ge(S["tab"], 5 * c + 5)
                act.activation(size, r, ACT.Abs).then_inc(S["sines"], 1)
                act.wait_ge(S["sines"], 3 * c + 1)
                act.activation(view(ring, c * SLOT + SIN_AT, D), r, ACT.Sin).then_inc(S["sines"], 1)
                act.activation(view(ring, c * SLOT + COS_AT, D), size, ACT.Sin, scale=-1.0, bias=halfpi[:, 0:1]).then_inc(S["sines"], 1)

            def square_piece(k):
                act.wait_ge(S["w_in"][k % 3], 16 * (k // 3 + 1))
                act.activation(piece_parts(k)[0], piece_in(k), ACT.Square,
                               accum_out=ssq[:, k:k + 1]).then_inc(S["ssq_ready"], 1)

            def high_piece(k):
                act.wait_ge(S["scale_ready"], k + 3)
                act.activation(piece_parts(k)[0], piece_in(k), ACT.Copy,
                               scale=scale[:, k:k + 1]).then_inc(S["hi_ready"], 1)

            for b in range(BATCH):
                def step_a(t, par, b=b):
                    if live(t, CHUNKS):
                        g = b * CHUNKS + t
                        act.wait_ge(S["xT_psum"], g + 1)
                        act.activation(view(ring, t * SLOT + X_AT, P).bitcast(F16), xT_bank[par][:, 0:D], ACT.Copy,
                                       scale=XS).then_inc(S["xhi_ready"], 1)
                    i = t - 1
                    if b == 0 and live(i, CHUNKS):
                        sines(i, 1 - par)
                    if live(i, CHUNKS):
                        g = b * CHUNKS + i
                        q = 1 - par
                        act.wait_ge(S["kv_psum"], g + 1)
                        need(act, S["rope_k"], 2 * (g - 1))
                        act.activation(act_k[:, q * D:(q + 1) * D], kv_bank[q][:, 0:D], ACT.Silu, scale=inv_p[:, :]).then_inc(S["k_act"], 1)
                        act.activation(view(ring, i * SLOT + V_AT, D), kv_bank[q][:, D:2 * D], ACT.Copy, scale=inv_p[:, :]).then_inc(S["v_ready"], 1)
                        act.activation(view(logits, g * EXPERTS, EXPERTS), lg_bank[q][:, 0:EXPERTS],
                                       ACT.Copy, scale=inv_p[:, :]).then_inc(S["lg_ready"], 1)
                    i = t - 2
                    if live(i, CHUNKS):
                        g = b * CHUNKS + i
                        act.wait_ge(S["kT_psum"], g + 1)
                        act.activation(view(ring, i * SLOT, 512), ps[3][:, :], ACT.Copy).then_inc(S["kT_ready"], 1)
                if b:
                    act.wait_ge(S["s_psum"], 2 * b * CHUNKS)
                    act.wait_ge(S["o_psum"], b * CHUNKS)
                    act.wait_ge(S["rope_q"], 2 * b * CHUNKS)
                else:
                    act.wait_ge(S["scale_ready"], 2)
                steps(act, CHUNKS, 0, 2, step_a)

                def step_b(t, par, b=b):
                    i = t - 1
                    if live(i, CHUNKS):
                        g = b * CHUNKS + i
                        q = 1 - par
                        act.wait_ge(S["qT_psum"], g + 1)
                        need(act, S["s_psum"], 2 * g)
                        for h in range(2):
                            act.activation(qbd[64 * h:64 * h + 64, :].rearrange("p (a h n) -> p a h n", a=4, h=2)[:, :, h, :],
                                           ps[0][64 * h:64 * h + 64, :].rearrange("p (a n) -> p a n", a=4),
                                           ACT.Copy).then_inc(S["q_moved"], 1)
                        need(act, S["o_psum"], g - 1)
                        act.activation(qT[:, q * 512:(q + 1) * 512], ps[0][:, :], ACT.Copy).then_inc(S["q_moved"], 1)
                    if live(t, CHUNKS):
                        g = b * CHUNKS + t
                        act.wait_ge(S["q_psum"], g + 1)
                        need(act, S["rope_q"], 2 * (g - 1))
                        act.activation(act_k[:, par * D:(par + 1) * D], ps[1 + par][:, 0:D], ACT.Silu, scale=inv_p[:, :]).then_inc(S["q_act"], 1)
                    for k in pieces_of(b, t - 1):
                        high_piece(k)
                    i = t - 2
                    if live(i, CHUNKS):
                        g = b * CHUNKS + i
                        act.wait_ge(S["o_psum"], g + 1)
                        need(act, S["z_ready"], 2 * g)
                        act.activation(oT, ps[5][:, 0:D], ACT.Copy).then_inc(S["o_moved"], 1)
                        need(act, S["ms_psum"], g)
                        act.activation(osq, ps[5][:, 0:D], ACT.Square).then_inc(S["o_moved"], 1)
                    for k in pieces_of(b, t):
                        act.wait_ge(S["o_psum"], b * CHUNKS + t - 1)
                        square_piece(k)
                    if b == BATCH - 1 and t >= DISPATCH_STEP - 1:
                        for r in rows_of(t + 1):
                            need(act, S["disp_out"][r % 4], 16 * (r // 4))
                            act.dma_start(row_bufs[r % 4][:, 0:D], xn_d[r * P:(r + 1) * P, :]).then_inc(S["disp_in"][r % 4], 16)
                act.wait_ge(S["rope_k"], 2 * (b + 1) * CHUNKS)
                act.wait_ge(S["gp_const"], 10)
                if b < BATCH - 1:
                    steps(act, CHUNKS, 0, 2, step_b)
                else:
                    step_b(0, 0)
                    step_b(1, 1)
                    act.wait_ge(S["route_a"], 8)
                    act.activation(spare[:, 320:576], spare[:, 64:320], ACT.Exp).then_inc(S["route_act"], 1)
                    for q in range(2):
                        act.wait_ge(S["xn_out"][q], 8 * TILES)
                    act.wait_ge(S["kv_psum"], TILES)
                    for t in range(2, CHUNKS + 3):
                        step_b(t, t & 1)

            act.wait_ge(S["o_psum"], TILES)
            for k in range(PIECES - 2, PIECES):
                square_piece(k)
            for k in range(PIECES - 2, PIECES):
                high_piece(k)

            def step(t, m):
                if live(t, SORTED):
                    act.wait_ge(S["xt_psum"], t + 1)
                    need(act, S["h_rows_psum"], 2 * (t - 1))
                    act.activation(moe_x[m % 2][:, 0:D], ps[0][:, 0:D], ACT.Copy, scale=XS).then_inc(S["moe_xhi"], 1)
                    if isinstance(t, int) and t == 0:
                        act.wait_ge(S["lo_ready"], PIECES - 1)
                        act.dma_start(b2_rows, b2[0:1, :].broadcast_to([P, EXPERTS * D])).then_inc(S["b_late"], 16)
                i = t - 2
                if live(i, SORTED):
                    for n in range(2):
                        act.wait_ge(S["h_ready"], 2 * i + n + 1)
                        need(act, S["ye_psum"], i - 1)
                        act.activation(moe_hh[m % 2][:, n * 512:(n + 1) * 512], moe_h[:, n * 512:(n + 1) * 512],
                                       ACT.Relu).then_inc(S["hhi_ready"], 1)
                i = t - 4
                if live(i, SORTED):
                    k, r = m % 4, (m - 4) % MOE_ROWS
                    act.wait_ge(S["y_summed"], i + 1)
                    need(act, S["ye_out"][k], 4 * (i - k))
                    act.activation(moe_y[k], moe_s, ACT.Copy, scale=moe_rows[r][:, D:D + 1]).then_inc(S["ye_ready"], 1)
                i = t - 1
                if live(i, SORTED):
                    for n in range(2):
                        act.wait_ge(S["h_rows_psum"], 2 * i + n + 1)
                        need(act, S["h_psum"], 2 * i - 1 + n)
                        act.activation(moe_h_rows[:, n * 512:(n + 1) * 512], ps[1 + n][:, :],
                                       ACT.Copy).then_inc(S["h_rows_ready"], 1)
            moe_steps(act, 4, step)

        @block.vector
        def _(dve):
            v = nc.vector
            T = S["tab"]

            def first_statistics(b):
                for t in range(2):
                    statistics(b, t, t)
                    dve.wait_ge(S["stat"], 2 * (b * CHUNKS + t) + 1)
                    variance(b, t, t)

            def reduce_angles(part, c, par):
                far, r = view(ring, c * SLOT + SIN_AT, D), angle_now[par]
                if part == 0:
                    dve.wait_ge(S["angle"], c + 1)
                    v.tensor_scalar(turns, far, float(1 / (2 * np.pi)), ROUND, ALU.mult, ALU.add).then_inc(T, 1)
                elif part == 1:
                    dve.wait_ge(T, 5 * c + 1)
                    v.tensor_scalar(turns, turns, ROUND, None, ALU.subtract).then_inc(T, 1)
                elif part == 2:
                    dve.wait_ge(T, 5 * c + 2)
                    need(dve, S["sines"], 3 * c - 3)
                    v.scalar_tensor_tensor(r, turns, -TWO_PI_A, far, ALU.mult, ALU.add).then_inc(T, 1)
                elif part == 3:
                    dve.wait_ge(T, 5 * c + 3)
                    v.scalar_tensor_tensor(r, turns, -TWO_PI_B, r, ALU.mult, ALU.add).then_inc(T, 1)
                else:
                    dve.wait_ge(T, 5 * c + 4)
                    v.tensor_scalar(r, r, PI_IN, -PI_IN, ALU.min, ALU.max).then_inc(T, 1)

            E = S["scale_step"]
            count = [0]

            def chain(ins):
                count[0] += 1
                ins.then_inc(E, 1)
                dve.wait_ge(E, count[0])

            def power(total, e, up, down, done=None):
                chain(v.tensor_scalar(e, total.bitcast(I32), 23, None, ALU.logical_shift_right))
                chain(v.tensor_scalar(e, e, 3.0, None, ALU.add))
                chain(v.tensor_scalar(e, e, 1, None, ALU.logical_shift_right))
                chain(v.tensor_scalar(up.bitcast(I32), e, -1.0, 206.0, ALU.mult, ALU.add))
                chain(v.tensor_scalar(up.bitcast(I32), up.bitcast(I32), 23, None, ALU.logical_shift_left))
                chain(v.tensor_scalar(e, e, 48.0, None, ALU.add))
                last = v.tensor_scalar(down.bitcast(I32), e, 23, None, ALU.logical_shift_left)
                if done is None:
                    chain(last)
                else:
                    last.then_inc(done, 1)

            def routing(part):
                A, F = S["route_a"], S["pad_step"]

                def cols(a, n):
                    return spare[:, a:a + n]

                def by_tile(ap):
                    return ap.rearrange("p (t e) -> p t e", e=EXPERTS)

                def per_tile(ap):
                    return ap.rearrange("p (t a) -> p t a", a=1).broadcast_to([P, TILES, EXPERTS])

                TE = TILES * EXPERTS
                top, less, ex = cols(32, TILES), cols(64, TE), cols(320, TE)
                pick, rank, red, onehot = cols(576, TE), cols(832, EXPERTS), cols(840, TILES), cols(872, TE)
                one, padded, ends, over = cols(1128, TILES), cols(1168, EXPERTS), cols(1176, EXPERTS), cols(1184, SORTED * EXPERTS)
                passed = cols(1500, SORTED)
                count_f, till, before, pad_sum = (cols(1544 + 8 * n, EXPERTS) for n in range(4))
                pad_over = cols(1576, PADS * EXPERTS)
                incl = pick
                L = by_tile(logits[:, :])
                i3 = incl.rearrange("p (e t) -> p e t", e=EXPERTS)
                whole = exp_of[:, 0:EXPERTS]
                if part == 0:
                    dve.wait_ge(S["lg_ready"], TILES)
                    for q in range(2):
                        dve.wait_ge(S["xn_out"][q], 8 * TILES)
                    v.reduce_max(top, L, AX.X).then_inc(A, 1)
                    for e in range(EXPERTS):
                        ins = v.memset(rank[:, e:e + 1], float(EXPERTS - e))
                    ins.then_inc(A, 1)
                    dve.wait_ge(A, 2)
                    v.tensor_tensor(by_tile(less), L, per_tile(top), ALU.subtract).then_inc(A, 1)
                    v.tensor_tensor(by_tile(pick), L, per_tile(top), ALU.is_equal).then_inc(A, 1)
                    dve.wait_ge(A, 4)
                    v.tensor_tensor(by_tile(pick), by_tile(pick),
                                    rank.rearrange("p (a e) -> p a e", a=1).broadcast_to([P, TILES, EXPERTS]), ALU.mult).then_inc(A, 1)
                    dve.wait_ge(A, 5)
                    v.reduce_max(red, by_tile(pick), AX.X).then_inc(A, 1)
                    dve.wait_ge(A, 6)
                    v.tensor_tensor(onehot.rearrange("p (e t) -> p t e", e=EXPERTS), by_tile(pick), per_tile(red),
                                    ALU.is_equal).then_inc(A, 1)
                    v.memset(one, 1.0).then_inc(A, 1)
                if part == 1:
                    dve.wait_ge(A, 8)
                    dve.wait_ge(S["route_pe"], 1)
                    for e in range(EXPERTS):
                        ins = v.tensor_tensor_scan(incl[:, e * TILES:(e + 1) * TILES], one,
                                                   ps[7][:, TE + e * TILES:TE + (e + 1) * TILES], 0.0, ALU.mult, ALU.add)
                    ins.then_inc(A, 1)
                    dve.wait_ge(A, 9)
                    v.tensor_scalar(whole, i3[:, :, TILES - 1], float(P - 1), None, ALU.add).then_inc(A, 1)
                    v.tensor_copy(count_f, i3[:, :, TILES - 1]).then_inc(F, 1)
                    dve.wait_ge(A, 10)
                    dve.wait_ge(F, 1)
                    v.tensor_tensor(incl, incl, ps[7][:, TE:2 * TE], ALU.subtract).then_inc(A, 1)
                    dve.wait_ge(A, 11)
                    shift = P.bit_length() - 1
                    v.tensor_scalar(whole, whole, shift, shift, ALU.logical_shift_right, ALU.logical_shift_left).then_inc(A, 1)
                    v.tensor_tensor(incl, incl, ps[7][:, 0:TE], ALU.add).then_inc(A, 1)
                if part == 2:
                    dve.wait_ge(A, 13)
                    v.tensor_copy(padded, whole).then_inc(A, 1)
                    dve.wait_ge(A, 14)
                    v.tensor_tensor_scan(ends, one[:, 0:EXPERTS], padded, 0.0, ALU.mult, ALU.add).then_inc(A, 1)
                    dve.wait_ge(A, 15)
                    v.tensor_tensor(padded, ends, padded, ALU.subtract).then_inc(A, 1)
                    dve.wait_ge(A, 16)
                    v.tensor_tensor(i3, i3, padded.rearrange("p (e a) -> p e a", a=1).broadcast_to([P, EXPERTS, TILES]),
                                    ALU.add).then_inc(A, 1)
                    dve.wait_ge(A, 17)
                    v.tensor_tensor(incl, incl, onehot, ALU.mult).then_inc(A, 1)
                    dve.wait_ge(A, 18)
                    v.reduce_sum(red, incl.rearrange("p (e t) -> p t e", e=EXPERTS), AX.X).then_inc(A, 1)
                    dve.wait_ge(S["gp_const"], 13)
                    v.tensor_tensor(over.rearrange("p (j e) -> p j e", e=EXPERTS),
                                    ends.rearrange("p (a e) -> p a e", a=1).broadcast_to([P, SORTED, EXPERTS]),
                                    starts[:, :].rearrange("p (j a) -> p j a", a=1).broadcast_to([P, SORTED, EXPERTS]),
                                    ALU.is_le).then_inc(A, 1)
                    dve.wait_ge(A, 20)
                    v.tensor_copy(posi[:, :], red).then_inc(A, 1)
                    v.reduce_sum(passed, over.rearrange("p (j e) -> p j e", e=EXPERTS), AX.X).then_inc(A, 1)
                    dve.wait_ge(A, 22)
                    v.tensor_scalar(exp_of[:, :], passed, float(EXPERTS - 1), None, ALU.min).then_inc(S["route_b"], 1)
                if part == 3:
                    v.tensor_tensor_scan(till, one[:, 0:EXPERTS], count_f, 0.0, ALU.mult, ALU.add).then_inc(F, 1)
                    dve.wait_ge(F, 2)
                    v.tensor_tensor(before, padded, till, ALU.subtract).then_inc(F, 1)
                    dve.wait_ge(F, 3)
                    v.tensor_tensor(before, before, count_f, ALU.add).then_inc(F, 1)
                    dve.wait_ge(F, 4)
                    po = pad_over.rearrange("p (j e) -> p j e", e=EXPERTS)
                    v.tensor_tensor(po, before.rearrange("p (a e) -> p a e", a=1).broadcast_to([P, PADS, EXPERTS]),
                                    pos0[:, 0:PADS].rearrange("p (j a) -> p j a", a=1).broadcast_to([P, PADS, EXPERTS]),
                                    ALU.is_le).then_inc(F, 1)
                    dve.wait_ge(F, 5)
                    v.tensor_tensor(po, po, count_f.rearrange("p (a e) -> p a e", a=1).broadcast_to([P, PADS, EXPERTS]),
                                    ALU.mult).then_inc(F, 1)
                    dve.wait_ge(F, 6)
                    v.reduce_sum(pad_sum[:, 0:PADS], po, AX.X).then_inc(F, 1)
                    dve.wait_ge(F, 7)
                    v.tensor_tensor(pad_sum[:, 0:PADS], pad_sum[:, 0:PADS], pos0[:, 0:PADS], ALU.add).then_inc(F, 1)
                    dve.wait_ge(F, 8)
                    v.tensor_copy(pad_posi[:, :], pad_sum[:, 0:PADS]).then_inc(S["route_b"], 1)
                    dve.wait_ge(S["route_act"], 1)
                    v.reduce_sum(red, by_tile(ex), AX.X).then_inc(A, 1)
                    dve.wait_ge(A, 23)
                    v.reciprocal(tag[:, 0::2], red).then_inc(S["route_b"], 1)

            def statistics(b, t, par):
                g = b * CHUNKS + t
                dve.wait_ge(S["x_in"][par], 8 * (g - par) + 16)
                v.bn_stats(st6[:, 6 * par:6 * par + 6], view(xy, t * D, D)).then_inc(S["stat"], 1)

            def variance(b, t, par):
                g = b * CHUNKS + t
                v.bn_aggr(mv[:, 2 * par:2 * par + 2], st6[:, 6 * par:6 * par + 6]).then_inc(S["stat"], 1)
                dve.wait_ge(S["stat"], 2 * g + 2)
                need(dve, S["rstd_ready"], g - 1)
                v.tensor_scalar(vare[:, par:par + 1], mv[:, 2 * par + 1:2 * par + 2], LN_EPS, None, ALU.add).then_inc(S["var_ready"], 1)

            def rope(src, dst, c, done):
                d4 = dst.rearrange("p (h s d) -> p h s d", h=HEADS, s=2)
                s3 = src.rearrange("p (h d) -> p h d", d=HD)
                for n, at_col in enumerate((COS_AT, SIN_AT)):
                    v.tensor_tensor(d4[:, :, n, :], s3, view(ring, c * SLOT + at_col, D).rearrange("p (h d) -> p h d", d=HD),
                                    ALU.mult).then_inc(done, 1)

            dve.wait_ge(S["tot_ready"], 1)
            pr = slice(PIECES, PIECES + 1)
            power(tot[:, pr], expo[:, pr], scale[:, pr], inv[:, pr])
            v.tensor_scalar(inv_p[:, :], inv[:, pr], 1.0 / XS, None, ALU.mult).then_inc(S["scale_ready"], 1)
            dve.wait_ge(S["gp_const"], 9)
            v.tensor_scalar(ones_s[:, :], ones[:, :], scale[:, pr], XS, ALU.mult, ALU.mult).then_inc(S["scale_ready"], 1)
            first_statistics(0)
            M = S["mask_part"]
            dve.wait_ge(S["es_ready"], 1)
            v.tensor_tensor(zT[:, 0:P], upper[:, :], ident[:, :], ALU.add).then_inc(M, 1)
            v.tensor_scalar(slope_bc[:, :], es[:, :], -1.0, None, ALU.add).then_inc(M, 1)
            dve.wait_ge(M, 2)
            for h in range(HEADS):
                ins = v.tensor_scalar(mask[:, h * P:(h + 1) * P], zT[:, 0:P], slope_bc[:, h:h + 1], 1.0, ALU.mult, ALU.add)
            ins.then_inc(S["rows"], 1)
            v.tensor_copy(es_row[:, :].rearrange("p (h d) -> p h d", d=HD),
                          es[:, :].rearrange("p (h a) -> p h a", a=1).broadcast_to([P, HEADS, HD])).then_inc(S["rows"], 1)
            dve.wait_ge(S["rows"], 2)
            dve.wait_ge(S["const_in"], 64)
            dve.wait_ge(S["es_ready"], 2)
            b1_tot, h_tot, h_up, h_down, s1, s2 = (hsc[:, a * 8:(a + 1) * 8] for a in range(1, 7))
            chain(v.tensor_tensor(b1_sq, b1_cols[:, :], b1_cols[:, :], ALU.mult))
            v.reduce_sum(hsc[:, 0:8], b1_sq.rearrange("p (e f) -> p e f", f=FC), AX.X).then_inc(S["b1_sum"], 2)
            dve.wait_ge(S["hi_ready"], 1)
            v.scalar_tensor_tensor(w_lo, stg[:, 0:2 * PCOLS], scale[:, pr], w_hi, ALU.mult, ALU.subtract).then_inc(S["lo_ready"], 1)

            def scale_piece(k):
                dve.wait_ge(S["tot_ready"], k + 2)
                power(tot[:, k:k + 1], expo[:, k:k + 1], scale[:, k:k + 1], inv[:, k:k + 1], S["scale_ready"])

            def low_piece(k):
                hi, lo = piece_parts(k)
                dve.wait_ge(S["hi_ready"], k + 2)
                v.scalar_tensor_tensor(lo, piece_in(k), scale[:, k:k + 1], hi,
                                       ALU.mult, ALU.subtract).then_inc(S["lo_ready"], 1)

            for b in range(BATCH):
                def step_a(t, par, b=b):
                    i = t + 2
                    measured = live(i, CHUNKS) and not (isinstance(t, int) and i < 2)
                    tables = b == 0 and live(t, CHUNKS)
                    if measured:
                        statistics(b, i, par)
                    if tables:
                        reduce_angles(0, t, par)
                    if measured:
                        dve.wait_ge(S["stat"], 2 * (b * CHUNKS + i) + 1)
                    i = t + 1
                    if live(i, CHUNKS):
                        g = b * CHUNKS + i
                        q = 1 - par
                        dve.wait_ge(S["rstd_ready"], g + 1)
                        need(dve, S["xT_psum"], g - 1)
                        need(dve, S["xn_out"][q], 8 * (g - q))
                        v.tensor_scalar(xn[:, q * D:(q + 1) * D], view(xy, i * D, D), mv[:, 2 * q:2 * q + 1], rstd[:, q:q + 1],
                                        ALU.subtract, ALU.mult).then_inc(S["xn_ready"], 1)
                    if measured:
                        variance(b, t + 2, par)
                    if tables:
                        reduce_angles(1, t, par)
                    if live(t, CHUNKS):
                        g = b * CHUNKS + t
                        xh = view(ring, t * SLOT + X_AT, D).bitcast(F16)
                        dve.wait_ge(S["xhi_ready"], g + 1)
                        v.scalar_tensor_tensor(xh[:, D:2 * D], xT_bank[par][:, 0:D], XS, xh[:, 0:D],
                                               ALU.mult, ALU.subtract).then_inc(S["xlo_ready"], 1)
                    if tables:
                        reduce_angles(2, t, par)
                    i = t - 1
                    if live(i, CHUNKS):
                        g = b * CHUNKS + i
                        q = 1 - par
                        dve.wait_ge(S["k_act"], g + 1)
                        need(dve, S["state_psum"], g - 1)
                        if b == 0:
                            dve.wait_ge(S["sines"], 3 * i + 3)
                        rope(act_k[:, q * D:(q + 1) * D], rot[:, q * 512:(q + 1) * 512], i, S["rope_k"])
                    if tables:
                        reduce_angles(3, t, par)
                    i = t - 2
                    if live(i, CHUNKS):
                        g = b * CHUNKS + i
                        dve.wait_ge(S["state_psum"], g + 1)
                        need(dve, S["state_ready"], 2 * g)
                        for h in range(2):
                            lo, hi = 64 * h, 64 * h + 64
                            one = ps[4][lo:hi, :].rearrange("p (g a c) -> p g a c", g=2, a=4)[:, :, 0:4:3, 32 * h:32 * h + 32]
                            before = region[lo:hi, bass.ds(i * SLOT + STATE_AT, D)].rearrange("p (g a c) -> p g a c", g=2, a=2)[:, :, :, 32 * h:32 * h + 32]
                            after = region[lo:hi, bass.ds((i + 1) * SLOT + STATE_AT, D)].rearrange("p (g a c) -> p g a c", g=2, a=2)[:, :, :, 32 * h:32 * h + 32]
                            v.tensor_tensor(after, one, before, ALU.add).then_inc(S["state_ready"], 1)
                    if tables:
                        reduce_angles(4, t, par)
                if b:
                    dve.wait_ge(S["w_ready"], b * CHUNKS)
                    dve.wait_ge(S["qT_psum"], b * CHUNKS)
                    dve.wait_ge(S["o_psum"], b * CHUNKS)
                steps(dve, CHUNKS, 2, 2, step_a)

                def step_b(t, par, b=b):
                    i = t - 3
                    if live(i, CHUNKS):
                        g = b * CHUNKS + i
                        q = 1 - par
                        dve.wait_ge(S["ms_psum"], g + 1)
                        need(dve, S["rms_ready"], g - 1)
                        v.tensor_scalar(mse[:, q:q + 1], ps[6][:, D:D + 1], 1.0 / D, RMS_EPS, ALU.mult, ALU.add).then_inc(S["ms_ready"], 1)
                    i = t - 2
                    if live(i, CHUNKS):
                        g = b * CHUNKS + i
                        need(dve, S["o_psum"], g - 1)
                        for n in range(2):
                            dve.wait_ge(S["s_psum"], 2 * g + n + 1)
                            v.tensor_tensor(masked[:, par * 1024 + n * 512:par * 1024 + (n + 1) * 512], ps[3 + n][:, :],
                                            mask[:, n * 512:(n + 1) * 512], ALU.mult).then_inc(S["s_masked"], 1)
                    if live(t, CHUNKS):
                        g = b * CHUNKS + t
                        dve.wait_ge(S["q_act"], g + 1)
                        need(dve, S["qT_psum"], g - 1)
                        rope(act_k[:, par * D:(par + 1) * D], rot[:, par * 512:(par + 1) * 512], t, S["rope_q"])
                    i = t - 2
                    if live(i, CHUNKS):
                        g = b * CHUNKS + i
                        dve.wait_ge(S["o_moved"], 2 * g + 1)
                        dve.wait_ge(S["u_psum"], g + 1)
                        need(dve, S["y_psum"], g)
                        for n in range(KC):
                            v.scalar_tensor_tensor(zT[:, n * P:(n + 1) * P], ps[6][:, n * P:(n + 1) * P],
                                                   inv_p[:, :], oT[:, n * P:(n + 1) * P],
                                                   ALU.mult, ALU.mult).then_inc(S["z_ready"], 1)
                    i = t - 3
                    if live(i, CHUNKS):
                        g = b * CHUNKS + i
                        q = 1 - par
                        dve.wait_ge(S["y_psum"], g + 1)
                        dve.wait_ge(S["rms_ready"], g + 1)
                        dve.wait_ge(S["xb_ready"], g + 1)
                        row = view(xy, i * D, D)
                        v.scalar_tensor_tensor(row, ps[7][:, 0:D], rms[:, q:q + 1], row, ALU.mult, ALU.add).then_inc(S["y_ready"], 1)
                    if b < BATCH - 1 and isinstance(t, int) and t == CHUNKS + 1:
                        first_statistics(b + 1)
                    for k in pieces_of(b, t - 1):
                        low_piece(k)
                    for k in pieces_of(b, t):
                        scale_piece(k)
                dve.wait_ge(S["state_psum"], (b + 1) * CHUNKS)
                if b < BATCH - 1:
                    steps(dve, CHUNKS, 0, 3, step_b)
                else:
                    for t in range(CHUNKS + 3):
                        step_b(t, t & 1)
                        for part in {0: (0,), 2: (1,), 3: (2, 3)}.get(t, ()):
                            routing(part)

            dve.wait_ge(S["o_psum"], TILES)
            scale_piece(PIECES - 2)
            h_e = expo[:, 0:EXPERTS]
            dve.wait_ge(S["b1_tot"], 1)
            chain(v.scalar_tensor_tensor(h_tot, tot[:, 0:PIECES:2], float(D), b1_tot, ALU.mult, ALU.add))
            chain(v.tensor_scalar(h_tot, h_tot, 2.0, None, ALU.mult))
            power(h_tot, h_e, h_up, h_down)
            dve.wait_ge(S["scale_ready"], PIECES + 1)
            chain(v.tensor_tensor(s1, inv[:, 0:PIECES:2], h_up, ALU.mult))
            chain(v.tensor_scalar(s1, s1, 1.0 / XS, None, ALU.mult))
            scale_piece(PIECES - 1)
            dve.wait_ge(S["scale_ready"], PIECES + 2)
            chain(v.tensor_tensor(s2, inv[:, 1:PIECES:2], h_down, ALU.mult))
            b3 = b1_cols[:, :].rearrange("p (e f) -> p e f", f=FC)
            chain(v.tensor_tensor(b3, b3, h_up.rearrange("p (e a) -> p e a", a=1).broadcast_to([P, EXPERTS, FC]), ALU.mult))
            for k in range(PIECES - 2, PIECES):
                low_piece(k)

            expert = {}

            def load_expert(i, slot):
                expert[slot] = nc.vector.value_load(exp_of[0:1, bass.ds(i, 1)], min_val=0, max_val=EXPERTS - 1)

            def begin(t, m):
                for d in (1, 2, 3, 4):
                    load_expert(t - d, (m - d) % MOE_ROWS)

            def step(t, m):
                i = t - 4
                if live(i, SORTED):
                    e, k, r = expert[(m - 4) % MOE_ROWS], m % 4, (m - 4) % MOE_ROWS
                    if isinstance(t, int) and i == 0:
                        dve.wait_ge(S["b_late"], 16)
                    dve.wait_ge(S["ye_psum"], i + 1)
                    need(dve, S["ye_ready"], i)
                    v.scalar_tensor_tensor(moe_s, ps[3 + m % 2][:, 0:D], view(s2, e, 1), view(b2_rows, e * D, D),
                                           ALU.mult, ALU.add).then_inc(S["y_summed"], 1)
                    need(dve, S["ye_out"][k], 4 * (i - k))
                    v.tensor_copy(ids[:, k:k + 1], moe_rows[r][:, D + 1:D + 2].bitcast(U32)).then_inc(S["ids_ready"], 1)
                if live(t, SORTED):
                    dve.wait_ge(S["moe_xhi"], t + 1)
                    v.scalar_tensor_tensor(moe_x[m % 2][:, D:2 * D], ps[0][:, 0:D], XS, moe_x[m % 2][:, 0:D],
                                           ALU.mult, ALU.subtract).then_inc(S["moe_xlo"], 1)
                i = t - 2
                if live(i, SORTED):
                    e = expert[(m - 2) % MOE_ROWS]
                    hh = moe_hh[m % 2]
                    for n in range(2):
                        dve.wait_ge(S["h_psum"], 2 * i + n + 1)
                        need(dve, S["hlo_ready"], 2 * i)
                        bias = view(b1_cols, e * FC + 4 * n, 4).rearrange("p (f a) -> p f a", a=1).broadcast_to([P, 4, P])
                        v.scalar_tensor_tensor(moe_h[:, n * 512:(n + 1) * 512].rearrange("p (f n) -> p f n", f=4),
                                               ps[5 + n][:, :].rearrange("p (f n) -> p f n", f=4), view(s1, e, 1), bias,
                                               ALU.mult, ALU.add).then_inc(S["h_ready"], 1)
                    for n in range(2):
                        dve.wait_ge(S["hhi_ready"], 2 * i + n + 1)
                        v.scalar_tensor_tensor(hh[:, 1024 + n * 512:1024 + (n + 1) * 512], moe_h[:, n * 512:(n + 1) * 512], 0.0,
                                               hh[:, n * 512:(n + 1) * 512], ALU.max, ALU.subtract).then_inc(S["hlo_ready"], 1)
                if live(t, SORTED):
                    load_expert(t, m)
            moe_steps(dve, 4, step, begin)

        @block.tensor
        def _(pe):
            mm = nc.tensor.matmul
            pe.wait_ge(S["gp_const"], 8)
            pe.wait_ge(S["const_in"], 64)
            pe.wait_ge(S["bias_in"], 64)
            pe.wait_ge(S["scale_ready"], 2)
            pe.wait_ge(S["lo_ready"], 1)

            def split_mm(dst, pairs, first, last):
                n = 0
                for (sh, sl), (mh, ml) in pairs:
                    for s, m in ((sh, mh), (sl, mh), (sh, ml)):
                        ins = mm(dst, s, m, start=first and n == 0, stop=last and n == 3 * len(pairs) - 1)
                        n += 1
                return ins

            def xpair(off, k):
                x16 = view(ring, off, D).bitcast(F16)
                return x16[:, k * P:(k + 1) * P], x16[:, D + k * P:D + (k + 1) * P]

            def wpair(k, lo, cols):
                return w_hi[:, k * PCOLS + lo:k * PCOLS + lo + cols], w_lo[:, k * PCOLS + lo:k * PCOLS + lo + cols]

            for b in range(BATCH):
                def step_a(t, par, b=b):
                    if live(t, CHUNKS):
                        g = b * CHUNKS + t
                        pe.wait_ge(S["xn_ready"], g + 1)
                        need(pe, S["xlo_ready"], g - 1)
                        for k in range(KC):
                            ins = nc.tensor.transpose(xT_bank[par][:, k * P:(k + 1) * P], xn[:, par * D + k * P:par * D + (k + 1) * P], ident[:, :])
                        ins.then_inc(S["xT_psum"], 1)
                    i = t - 1
                    if live(i, CHUNKS):
                        g = b * CHUNKS + i
                        pe.wait_ge(S["xlo_ready"], g + 1)
                        need(pe, S["lg_ready"], g - 1)
                        kv, lg = kv_bank[1 - par], lg_bank[1 - par]
                        mm(kv[:, :], ones_s[:, :], bias_p[:, 0:512], start=True, stop=False)
                        split_mm(kv[:, :], [(xpair(i * SLOT + X_AT, k), wpair(k, KV, 512)) for k in range(KC)], False, True)
                        split_mm(lg[:, 0:EXPERTS], [(xpair(i * SLOT + X_AT, k), wpair(k, RT, EXPERTS)) for k in range(KC)],
                                 True, True).then_inc(S["kv_psum"], 1)
                    i = t - 2
                    if live(i, CHUNKS):
                        g = b * CHUNKS + i
                        pe.wait_ge(S["rope_k"], 2 * g + 2)
                        need(pe, S["kT_ready"], g)
                        for a in range(4):
                            ins = nc.tensor.transpose(ps[3][:, a * P:(a + 1) * P], rot[:, par * 512 + a * P:par * 512 + (a + 1) * P], ident[:, :])
                        ins.then_inc(S["kT_psum"], 1)
                        pe.wait_ge(S["v_ready"], g + 1)
                        need(pe, S["state_ready"], 2 * g)
                        for a in range(4):
                            ins = mm(ps[4][:, a * P:(a + 1) * P], rot[:, par * 512 + a * P:par * 512 + (a + 1) * P],
                                     view(ring, i * SLOT + V_AT + (a // 2) * P, P), start=True, stop=True)
                        ins.then_inc(S["state_psum"], 1)
                if b:
                    pe.wait_ge(S["q_moved"], 3 * b * CHUNKS)
                    pe.wait_ge(S["q_act"], b * CHUNKS)
                    pe.wait_ge(S["s_masked"], 2 * b * CHUNKS)
                    pe.wait_ge(S["o_moved"], 2 * b * CHUNKS)
                    pe.wait_ge(S["z_ready"], 2 * b * CHUNKS)
                    pe.wait_ge(S["ms_ready"], b * CHUNKS)
                    pe.wait_ge(S["y_ready"], b * CHUNKS)
                steps(pe, CHUNKS, 0, 2, step_a)
                def step_b(t, par, b=b):
                    if isinstance(t, int) and t == 1:
                        pe.wait_ge(S["kT_ready"], (b + 1) * CHUNKS)
                        pe.wait_ge(S["state_ready"], 2 * (b + 1) * CHUNKS)
                    i = t - 1
                    q = 1 - par
                    if live(i, CHUNKS):
                        g = b * CHUNKS + i
                        pe.wait_ge(S["rope_q"], 2 * g + 2)
                        need(pe, S["q_moved"], 3 * g)
                        for a in range(4):
                            ins = nc.tensor.transpose(ps[0][:, a * P:(a + 1) * P], rot[:, q * 512 + a * P:q * 512 + (a + 1) * P], ident[:, :])
                        ins.then_inc(S["qT_psum"], 1)
                    i = t - 3
                    if live(i, CHUNKS):
                        g = b * CHUNKS + i
                        pe.wait_ge(S["z_ready"], 2 * g + 2)
                        pe.wait_ge(S["o_moved"], 2 * g + 2)
                        for k in range(KC):
                            ins = mm(ps[6][:, D:D + 96], osq[:, k * P:(k + 1) * P], ones[:, 0:96],
                                     start=k == 0, stop=k == KC - 1)
                        ins.then_inc(S["ms_psum"], 1)
                        need(pe, S["y_ready"], g)
                        if b == BATCH - 1 and t == 3:
                            pe.wait_ge(S["route_a"], 13)
                        for k in range(KC):
                            ins = mm(ps[7][:, 0:D], zT[:, k * P:(k + 1) * P], wo_sb[:, k * D:(k + 1) * D],
                                     start=k == 0, stop=k == KC - 1)
                        ins.then_inc(S["y_psum"], 1)
                    if live(t, CHUNKS):
                        g = b * CHUNKS + t
                        need(pe, S["q_act"], g - 1)
                        mm(ps[1 + par][:, 0:D], ones_s[:, :], bias_p[:, 512:768], start=True, stop=False)
                        split_mm(ps[1 + par][:, 0:D], [(xpair(t * SLOT + X_AT, k), wpair(k, Q, D)) for k in range(KC)],
                                 False, True).then_inc(S["q_psum"], 1)
                    i = t - 2
                    if live(i, CHUNKS):
                        g = b * CHUNKS + i
                        need(pe, S["z_ready"], 2 * g)
                        need(pe, S["ms_ready"], g)
                        for n in range(KC):
                            mm(ps[6][:, n * P:(n + 1) * P], bias_p[:, 768 + n * P:768 + (n + 1) * P], ones_s[:, :], start=True, stop=False)
                            ins = split_mm(ps[6][:, n * P:(n + 1) * P],
                                           [(wpair(k, U + n * P, P), xpair(i * SLOT + X_AT, k)) for k in range(KC)], False, True)
                        ins.then_inc(S["u_psum"], 1)
                        pe.wait_ge(S["v_now"], 16 * g + 16)
                        pe.wait_ge(S["w_ready"], g + 1)
                        need(pe, S["o_moved"], 2 * g)
                        pe.wait_ge(S["q_moved"], 3 * g + 3)
                        pe.wait_ge(S["s_masked"], 2 * g + 2)
                        for n in range(2):
                            for a in range(2):
                                pair = 2 * n + a
                                mm(ps[5][64 * a:64 * a + 64, n * P:(n + 1) * P], w_now[:, par * D + pair * 64:par * D + (pair + 1) * 64],
                                   qT[:, par * 512 + pair * P:par * 512 + (pair + 1) * P], start=True, stop=False, skip_group_check=True)
                            for hh in range(4):
                                h = 4 * n + hh
                                ins = mm(ps[5][32 * hh:32 * hh + 32, n * P:(n + 1) * P], v_now[:, h * HD:(h + 1) * HD],
                                         masked[:, par * 1024 + h * P:par * 1024 + (h + 1) * P], start=False, stop=True,
                                         skip_group_check=True)
                        ins.then_inc(S["o_psum"], 1)
                    i = t - 1
                    if live(i, CHUNKS):
                        g = b * CHUNKS + i
                        pe.wait_ge(S["q_moved"], 3 * g + 2)
                        pe.wait_ge(S["k_now"], 16 * g + 16)
                        for n in range(2):
                            need(pe, S["s_masked"], 2 * g - 1 + n)
                            for a in range(2):
                                pair = 2 * n + a
                                ins = mm(ps[3 + n][:, a * D:(a + 1) * D], kT_now[:, pair * P:(pair + 1) * P],
                                         qbd[:, pair * D:(pair + 1) * D], start=True, stop=True)
                            ins.then_inc(S["s_psum"], 1)
                pe.wait_ge(S["lg_ready"], (b + 1) * CHUNKS)
                if b < BATCH - 1:
                    steps(pe, CHUNKS, 0, 3, step_b)
                else:
                    step_b(0, 0)
                    step_b(1, 1)
                    pe.wait_ge(S["route_a"], 7)
                    te = TILES * EXPERTS
                    mm(ps[7][:, 0:te], upper[:, :], spare[:, 872:872 + te], start=True, stop=True)
                    mm(ps[7][:, te:2 * te], ones[:, :], spare[:, 872:872 + te], start=True, stop=True).then_inc(S["route_pe"], 1)
                    for t in range(2, CHUNKS + 3):
                        step_b(t, t & 1)

            pe.wait_ge(S["y_ready"], TILES)

            expert = {}

            def load_expert(i, slot):
                expert[slot] = nc.tensor.value_load(exp_of[0:1, bass.ds(i, 1)], min_val=0, max_val=EXPERTS - 1)

            def begin(t, m):
                for d in (1, 2, 3):
                    load_expert(t - d, (m - d) % MOE_ROWS)

            r16 = region[:, :].bitcast(F16)

            def step(t, m):
                if live(t, SORTED):
                    pe.wait_ge(S["xs_in"][m], 2 * (t - m) + 16)
                    need(pe, S["moe_xlo"], t)
                    for k in range(KC):
                        ins = nc.tensor.transpose(ps[0][:, k * P:(k + 1) * P], moe_rows[m][:, k * P:(k + 1) * P], ident[:, :])
                    ins.then_inc(S["xt_psum"], 1)
                i = t - 2
                if live(i, SORTED):
                    for n in range(2):
                        pe.wait_ge(S["h_rows_ready"], 2 * i + n + 1)
                        need(pe, S["h_ready"], 2 * i - 1 + n)
                        for f in range(4):
                            ins = nc.tensor.transpose(ps[5 + n][:, f * P:(f + 1) * P],
                                                      moe_h_rows[:, (4 * n + f) * P:(4 * n + f + 1) * P], ident[:, :])
                        ins.then_inc(S["h_psum"], 1)
                i = t - 1
                if live(i, SORTED):
                    if isinstance(t, int) and t <= 3:
                        pe.wait_ge(S["lo_ready"], 1 + PIECES)
                        load_expert(i, m - 1)
                    e = expert[(m - 1) % MOE_ROWS]
                    xh = moe_x[(m - 1) % 2]
                    pe.wait_ge(S["moe_xlo"], i + 1)
                    for n in range(2):
                        need(pe, S["h_rows_ready"], 2 * i - 1 + n)
                        pairs = [((xh[:, k * P:(k + 1) * P], xh[:, D + k * P:D + (k + 1) * P]),
                                  (view(r16, e * 4 * WPIECE + k * FF + n * 512, 512),
                                   view(r16, e * 4 * WPIECE + WPIECE + k * FF + n * 512, 512))) for k in range(KC)]
                        split_mm(ps[1 + n][:, :], pairs, True, True).then_inc(S["h_rows_psum"], 1)
                i = t - 3
                if live(i, SORTED):
                    e = expert[(m - 3) % MOE_ROWS]
                    hh = moe_hh[(m - 3) % 2]
                    need(pe, S["y_summed"], i - 1)
                    pe.wait_ge(S["hlo_ready"], 2 * i + 2)
                    pairs = [((hh[:, f * P:(f + 1) * P], hh[:, 1024 + f * P:1024 + (f + 1) * P]),
                              (view(r16, (e * 4 + 2) * WPIECE + f * D, D), view(r16, (e * 4 + 3) * WPIECE + f * D, D)))
                             for f in range(FC)]
                    bank = ps[3 + (m - 3) % 2]
                    split_mm(bank[:, 0:D], pairs[0:2], True, False)
                    if live(t, SORTED):
                        load_expert(t, m)
                    split_mm(bank[:, 0:D], pairs[2:], False, True).then_inc(S["ye_psum"], 1)
            moe_steps(pe, 3, step, begin)


def kernel(**inputs):
    import concourse.bacc as bacc
    from concourse.bass_utils import run_bass_kernel_spmd

    g = {n: np.asarray(a) for n, a in inputs.items()}
    wt = g["L0_attn_qkvu_w"].T
    q, k, v, u = (wt[:, n * D:(n + 1) * D] for n in range(4))
    proj = np.concatenate([k, v, g["L0_ffn_w_router"], q, u], axis=1)
    bq, bk, bv, bu = (g["L0_attn_qkvu_b"][n * D:(n + 1) * D] for n in range(4))

    def rows(w, chunks):
        return w.reshape(chunks, P, -1).transpose(1, 0, 2).reshape(P, -1)

    w1 = g["L0_ffn_w1"].reshape(EXPERTS, KC, P, FF).transpose(2, 0, 1, 3).reshape(P, EXPERTS, WPIECE)
    w2 = g["L0_ffn_w2"].reshape(EXPERTS, FC, P, D).transpose(2, 0, 1, 3).reshape(P, EXPERTS, WPIECE)
    arrays = {
        "x": g["L0_attn_x"].reshape(-1, D), "slope": g["L0_attn_slope_rate"].reshape(1, HEADS),
        "wqkvu": rows(proj, KC), "bqkvu": np.concatenate([bk, bv, bq, bu]).reshape(-1, P), "wout": rows(g["L0_attn_out_w"].T, KC),
        "bout": g["L0_attn_out_b"][None], "theta": g["L0_attn_theta"].reshape(1, D),
        "wexp": np.stack([w1, w2], axis=2).reshape(P, -1),
        "b1": g["L0_ffn_b1"].reshape(EXPERTS, FC, P).transpose(2, 0, 1).reshape(P, -1),
        "b2": g["L0_ffn_b2"].reshape(1, -1),
    }
    arrays = {n: np.ascontiguousarray(a) for n, a in arrays.items()}
    nc = bacc.Bacc("TRN2", target_bir_lowering=False, num_devices=1)
    args = [nc.dram_tensor(n, a.shape, mybir.dt.from_np(a.dtype), kind="ExternalInput").ap() for n, a in arrays.items()]
    out = nc.dram_tensor("out", (TILES * P, D), F32, kind="ExternalOutput").ap()
    xn_d = nc.dram_tensor("xn_rows", (TILES * P, D), F32).ap()
    sorted_d = nc.dram_tensor("sorted_rows", (SORTED * P, ROW), F32).ap()
    build(nc, *args, out, xn_d, sorted_d)
    r = run_bass_kernel_spmd(nc, [arrays], core_ids=[0])
    return r.results[0]["out"].reshape(BATCH, SEQ, D)
```
